# Optimizing a Trainium2 kernel written in Bass

```python
import numpy as np
import jax
import jax.numpy as jnp

def _softmax(x, axis=-1):
    return jax.nn.softmax(x, axis=axis)

def _gelu(x):
    return jax.nn.gelu(x, approximate=True)

def _silu(x):
    return jax.nn.silu(x)

def _sigmoid(x):
    return jax.nn.sigmoid(x)

def _layernorm(x, axis=-1, eps=1e-05):
    m = jnp.mean(x, axis=axis, keepdims=True)
    v = jnp.var(x, axis=axis, keepdims=True)
    return (x - m) / jnp.sqrt(v + eps)

def _scatter_add(tgt, idx, src, axis=0):
    return tgt.at[idx].add(src)

def _segment_sum(src, seg, n):
    return jax.ops.segment_sum(src, seg, n)
kernel_name = 'mk_lm_tower_d2_tok_ids256_r4_c40352'

def setup_inputs(seed: int=0):
    np.random.seed(seed)
    _w = jnp.asarray

    def _rec_inputs():
        import jax
        import jax.numpy as jnp
        _rk = jax.random.key(seed)
        x = jax.random.randint(jax.random.fold_in(_rk, 1), (64, 128), 0, 250, jnp.int32)
        return x
    x = _rec_inputs()

    def _L0_tok_setup():
        import jax, jax.numpy as jnp
        import numpy as np
        B, T, H, VOCAB = (128, 128, 64, 250)
        EPS = 1e-12

        def _pos_graph(seq_inputs):
            si = seq_inputs[:, :, None]
            mask = si != 0
            equal = si == si.transpose(0, 2, 1)
            tril = jnp.tril(jnp.ones((si.shape[1], si.shape[1]), dtype=jnp.float32))
            rel = equal.astype(jnp.float32) * tril
            rel = rel * mask.astype(jnp.float32) * mask.transpose(0, 2, 1).astype(jnp.float32)
            norm = rel.sum(-2, keepdims=True)
            norm = jnp.where(norm == 0, 1.0, norm)
            return rel / norm

        def _get_pos_emb(seq_inputs, emb_table):
            seq_mask = seq_inputs != 0
            length = seq_mask.sum(1, keepdims=True)
            coo = jnp.arange(seq_inputs.shape[1])[None, :] * seq_mask
            pos_index = (length - coo) * seq_mask
            return emb_table[pos_index]
        key = jax.random.key(seed)
        k1, k2, k3, k4 = jax.random.split(key, 4)
        stdv = 1.0 / np.sqrt(H)
        seq_inputs = jax.random.randint(k1, (B, T), 0, VOCAB, dtype=jnp.int64 if jax.config.jax_enable_x64 else jnp.int32)
        emb_table = jax.random.normal(k2, (T + 1, H), dtype=jnp.float32)
        W_in = jax.random.uniform(k3, (H, H), minval=-stdv, maxval=stdv, dtype=jnp.float32)
        b_oah = jax.random.uniform(k4, (H,), minval=-stdv, maxval=stdv, dtype=jnp.float32)
        return {'seq_inputs': seq_inputs, 'emb_table': emb_table, 'W_in': W_in, 'b_oah': b_oah}
    _L0_tok_all = _L0_tok_setup()
    _L0_tok_in = {k: v for k, v in _L0_tok_all.items() if k in ('emb_table', 'W_in', 'b_oah')}
    del _L0_tok_all

    def _L0_attn_setup():
        import jax, jax.numpy as jnp
        import numpy as np
        SEQ, BATCH, IN, HID = (512, 64, 64, 64)
        key = jax.random.key(seed)
        k1, k2, k3, k4, k5 = jax.random.split(key, 5)
        s = 1.0 / np.sqrt(HID)
        return {'x_in': jax.random.normal(k1, (SEQ, BATCH, IN), dtype=jnp.float32), 'W_ih': jax.random.uniform(k2, (HID, IN), jnp.float32, -s, s), 'W_hh': jax.random.uniform(k3, (HID, HID), jnp.float32, -s, s), 'b_ih': jax.random.uniform(k4, (HID,), jnp.float32, -s, s), 'b_hh': jax.random.uniform(k5, (HID,), jnp.float32, -s, s)}
    _L0_attn_all = _L0_attn_setup()
    _L0_attn_in = {k: v for k, v in _L0_attn_all.items() if k in ('W_ih', 'W_hh', 'b_ih', 'b_hh')}
    del _L0_attn_all

    def _L0_ffn_setup():
        import jax, jax.numpy as jnp
        import numpy as np
        B, T, D, H, E = (16, 1024, 64, 128, 8)
        key = jax.random.key(seed)
        ks = jax.random.split(key, 5)
        x = jax.random.normal(ks[0], (B, T, D), dtype=jnp.float32)
        gate_w = jax.random.normal(ks[1], (D, E), dtype=jnp.float32) * 0.02
        gate_b = jnp.zeros((E,), dtype=jnp.float32)
        W1 = jax.random.normal(ks[2], (E, D, H), dtype=jnp.float32) * 0.02
        b1 = jnp.zeros((E, H), dtype=jnp.float32)
        W2 = jax.random.normal(ks[3], (E, H, D), dtype=jnp.float32) * 0.02
        b2 = jnp.zeros((E, D), dtype=jnp.float32)
        return {'x': x, 'gate_w': gate_w, 'gate_b': gate_b, 'W1': W1, 'b1': b1, 'W2': W2, 'b2': b2}
    _L0_ffn_all = _L0_ffn_setup()
    _L0_ffn_in = {k: v for k, v in _L0_ffn_all.items() if k in ('gate_w', 'gate_b', 'W1', 'b1', 'W2', 'b2')}
    del _L0_ffn_all

    def _L1_attn_setup():
        import jax, jax.numpy as jnp
        import numpy as np
        key = jax.random.key(seed)
        inputs = jax.random.normal(key, (8, 512, 64), dtype=jnp.float32)
        return {'inputs': inputs}
    _L1_attn_all = _L1_attn_setup()
    _L1_attn_in = {k: v for k, v in _L1_attn_all.items() if k in ()}
    del _L1_attn_all

    def _L1_ffn_setup():
        import jax, jax.numpy as jnp
        import numpy as np
        B, K, D = (128, 16, 64)
        E = 32
        H = int(D * 0.25)
        key = jax.random.key(seed)
        ks = jax.random.split(key, 7)
        d_rs = D ** (-0.5)
        h_rs = H ** (-0.5)
        x = jax.random.normal(ks[0], (B, K, D), dtype=jnp.float32)
        router_w = jax.random.uniform(ks[1], (E, D), jnp.float32, -d_rs, d_rs)
        router_b = jax.random.uniform(ks[2], (E,), jnp.float32, -d_rs, d_rs)
        W1 = jax.random.uniform(ks[3], (E, D, H), jnp.float32, -h_rs, h_rs)
        b1 = jax.random.uniform(ks[4], (E, H), jnp.float32, -h_rs, h_rs)
        W2 = jax.random.uniform(ks[5], (E, H, D), jnp.float32, -d_rs, d_rs)
        b2 = jax.random.uniform(ks[6], (E, D), jnp.float32, -d_rs, d_rs)
        return {'x': x, 'router_w': router_w, 'router_b': router_b, 'W1': W1, 'b1': b1, 'W2': W2, 'b2': b2}
    _L1_ffn_all = _L1_ffn_setup()
    _L1_ffn_in = {k: v for k, v in _L1_ffn_all.items() if k in ('router_w', 'router_b', 'W1', 'b1', 'W2', 'b2')}
    del _L1_ffn_all
    return {'x': x, 'L0_tok_emb_table': _L0_tok_in['emb_table'], 'L0_tok_W_in': _L0_tok_in['W_in'], 'L0_tok_b_oah': _L0_tok_in['b_oah'], 'L0_attn_W_ih': _L0_attn_in['W_ih'], 'L0_attn_W_hh': _L0_attn_in['W_hh'], 'L0_attn_b_ih': _L0_attn_in['b_ih'], 'L0_attn_b_hh': _L0_attn_in['b_hh'], 'L0_ffn_gate_w': _L0_ffn_in['gate_w'], 'L0_ffn_gate_b': _L0_ffn_in['gate_b'], 'L0_ffn_W1': _L0_ffn_in['W1'], 'L0_ffn_b1': _L0_ffn_in['b1'], 'L0_ffn_W2': _L0_ffn_in['W2'], 'L0_ffn_b2': _L0_ffn_in['b2'], 'L1_ffn_router_w': _L1_ffn_in['router_w'], 'L1_ffn_router_b': _L1_ffn_in['router_b'], 'L1_ffn_W1': _L1_ffn_in['W1'], 'L1_ffn_b1': _L1_ffn_in['b1'], 'L1_ffn_W2': _L1_ffn_in['W2'], 'L1_ffn_b2': _L1_ffn_in['b2']}

def reference(x, L0_tok_emb_table, L0_tok_W_in, L0_tok_b_oah, L0_attn_W_ih, L0_attn_W_hh, L0_attn_b_ih, L0_attn_b_hh, L0_ffn_gate_w, L0_ffn_gate_b, L0_ffn_W1, L0_ffn_b1, L0_ffn_W2, L0_ffn_b2, L1_ffn_router_w, L1_ffn_router_b, L1_ffn_W1, L1_ffn_b1, L1_ffn_W2, L1_ffn_b2):
    import jax
    import jax.numpy as jnp

    def _L0_tok_ref(seq_inputs, emb_table, W_in, b_oah):
        import jax, jax.numpy as jnp
        import numpy as np
        B, T, H, VOCAB = (128, 128, 64, 250)
        EPS = 1e-12

        def _pos_graph(seq_inputs):
            si = seq_inputs[:, :, None]
            mask = si != 0
            equal = si == si.transpose(0, 2, 1)
            tril = jnp.tril(jnp.ones((si.shape[1], si.shape[1]), dtype=jnp.float32))
            rel = equal.astype(jnp.float32) * tril
            rel = rel * mask.astype(jnp.float32) * mask.transpose(0, 2, 1).astype(jnp.float32)
            norm = rel.sum(-2, keepdims=True)
            norm = jnp.where(norm == 0, 1.0, norm)
            return rel / norm

        def _get_pos_emb(seq_inputs, emb_table):
            seq_mask = seq_inputs != 0
            length = seq_mask.sum(1, keepdims=True)
            coo = jnp.arange(seq_inputs.shape[1])[None, :] * seq_mask
            pos_index = (length - coo) * seq_mask
            return emb_table[pos_index]
        step = 1
        A_in = _pos_graph(seq_inputs)
        pe = _get_pos_emb(seq_inputs, emb_table)
        nrm = jnp.sqrt(jnp.sum(pe * pe, axis=1, keepdims=True))
        pe = pe / jnp.maximum(nrm, EPS)
        for _ in range(step):
            h_n = jnp.einsum('bth,oh->bto', pe, W_in)
            pe = jnp.einsum('bji,bjh->bih', A_in, h_n) + b_oah
        return pe

    def _L0_attn_ref(x_in, W_ih, W_hh, b_ih, b_hh):
        import jax, jax.numpy as jnp
        import numpy as np
        SEQ, BATCH, IN, HID = (512, 64, 64, 64)
        xp = jnp.einsum('tbi,hi->tbh', x_in, W_ih) + b_ih + b_hh
        h0 = jnp.zeros((x_in.shape[1], W_hh.shape[0]), dtype=x_in.dtype)

        def step(h, xp_t):
            h_new = jnp.tanh(xp_t + h @ W_hh.T)
            return (h_new, h_new)
        _, hiddens = jax.lax.scan(step, h0, xp)
        return hiddens

    def _L0_ffn_ref(x, gate_w, gate_b, W1, b1, W2, b2):
        import jax, jax.numpy as jnp
        import numpy as np
        B, T, D, H, E = (16, 1024, 64, 128, 8)
        Bb, Tt, Dd = x.shape
        Ee = gate_w.shape[1]
        xf = x.reshape(-1, Dd)
        N = xf.shape[0]
        logits = xf @ gate_w + gate_b
        probs = jax.nn.softmax(logits, axis=-1)
        top2_vals, top2_idx = jax.lax.top_k(probs, 2)
        cw = jnp.zeros((N, Ee), dtype=xf.dtype).at[jnp.arange(N)[:, None], top2_idx].add(top2_vals)

        def step(acc, params):
            w1, bb1, w2, bb2, we = params
            h = jax.nn.gelu(xf @ w1 + bb1, approximate=False)
            y = h @ w2 + bb2
            return (acc + we[:, None] * y, None)
        out, _ = jax.lax.scan(step, jnp.zeros_like(xf), (W1, b1, W2, b2, cw.T))
        return out.reshape(Bb, Tt, Dd)

    def _L1_attn_ref(inputs):
        import jax, jax.numpy as jnp
        import numpy as np
        d_k = jnp.asarray(inputs.shape[-1], dtype=inputs.dtype)
        scores = jnp.einsum('bnd,bmd->bnm', inputs, inputs) / jnp.sqrt(d_k)
        weights = jax.nn.softmax(scores, axis=-1)
        context = jnp.einsum('bnm,bmd->bnd', weights, inputs)
        return context

    def _L1_ffn_ref(x, router_w, router_b, W1, b1, W2, b2):
        import jax, jax.numpy as jnp
        import numpy as np
        B, K, D = (128, 16, 64)
        E = 32
        H = int(D * 0.25)
        xf = x.reshape(-1, D)
        logits = xf @ router_w.T + router_b
        idx = jnp.argmax(logits, axis=-1)
        w1t = jnp.take(W1, idx, axis=0)
        h = jnp.einsum('nd,ndh->nh', xf, w1t) + jnp.take(b1, idx, axis=0)
        h = jax.nn.relu(h)
        w2t = jnp.take(W2, idx, axis=0)
        out = jnp.einsum('nh,nhd->nd', h, w2t) + jnp.take(b2, idx, axis=0)
        out = jax.nn.relu(out)
        return out.reshape(x.shape)
    h = _L0_tok_ref(x, L0_tok_emb_table, L0_tok_W_in, L0_tok_b_oah)
    h = h + _L0_attn_ref(_layernorm(h, axis=-1), L0_attn_W_ih, L0_attn_W_hh, L0_attn_b_ih, L0_attn_b_hh)
    h = h + _L0_ffn_ref(_layernorm(h, axis=-1), L0_ffn_gate_w, L0_ffn_gate_b, L0_ffn_W1, L0_ffn_b1, L0_ffn_W2, L0_ffn_b2)
    h = h + _L1_attn_ref(_layernorm(h, axis=-1))
    h = h + _L1_ffn_ref(_layernorm(h, axis=-1), L1_ffn_router_w, L1_ffn_router_b, L1_ffn_W1, L1_ffn_b1, L1_ffn_W2, L1_ffn_b2)
    return h

_drawn_inputs = setup_inputs


def setup_inputs(seed=0):
    import zlib

    import numpy as np

    out = dict(_drawn_inputs(seed))
    spreads = {'L0_ffn_gate_b': (0.0, 0.1), 'L0_ffn_b1': (0.0, 0.356), 'L0_ffn_b2': (0.0, 0.1)}
    factors = {'L0_ffn_W2': 2.931, 'L1_ffn_b1': 4.287}
    for name, (base, spread) in spreads.items():
        noise = np.random.default_rng([zlib.crc32(name.encode()), seed]).standard_normal(out[name].shape)
        drawn = base * np.exp(spread * noise) if base else spread * noise
        out[name] = jnp.asarray(drawn.astype(out[name].dtype))
    for name, factor in factors.items():
        out[name] = (out[name] * factor).astype(out[name].dtype)
    return out
```

```python
import concourse.bass as bass
from concourse import mybir
from contextlib import ExitStack


def lm_tower_kernel(nc, tok, tok_cols, weights, diag_b2, emb_last, out, COLS):
    fp32, bf16, fp16, i32 = (mybir.dt.float32, mybir.dt.bfloat16, mybir.dt.float16, mybir.dt.int32)
    ALU = mybir.AluOpType
    ACT = mybir.ActivationFunctionType
    AX = mybir.AxisListType

    P = 128
    B, T = tok.shape
    D = 64
    HALF = P // 2
    VROWS = T + 1
    GS = 4
    NG = B // GS
    GT = GS * T
    GD = GS * D
    E1, H1 = 8, 128
    E2, H2 = 32, 16
    CH = E2 * H2 // P
    WS = 256.0
    BIG = 2.0 ** 100
    EPS_LN = 1e-5
    EPS_NORM_SQ = 1e-24
    LAG_N, LAG_R, LAG_M = 1, 2, 3

    ctx = ExitStack()
    with ctx:
        def sb(name, shape, dt):
            return ctx.enter_context(nc.sbuf_tensor(name, shape, dt))

        def bank(name):
            return ctx.enter_context(nc.psum_tensor(name, [P, 512], fp32))

        def sem(name):
            return ctx.enter_context(nc.semaphore(name))

        W = sb("W", [P, COLS["_total"]], fp32)

        def w(name):
            a, n = COLS[name]
            return W[:, a:a + n]

        emb129 = sb("emb129", [1, D], fp32)
        b2diag = sb("b2diag", [GS * E1, GD], fp32)
        whh_bd = sb("whh_bd", [P, P], fp32)
        rnn_bias = sb("rnn_bias", [P, 1], fp32)
        w1_hi = sb("w1_hi", [P, E1 * H1], fp16)
        w1_lo = sb("w1_lo", [P, E1 * H1], fp16)
        gate_hi = sb("gate_hi", [P, E1], fp16)
        gate_lo = sb("gate_lo", [P, E1], fp16)
        rout_hi = sb("rout_hi", [P, E2], fp16)
        rout_lo = sb("rout_lo", [P, E2], fp16)
        f1_hi = sb("f1_hi", [P, CH * P], fp16)
        f1_lo = sb("f1_lo", [P, CH * P], fp16)
        f1_pick = sb("f1_pick", [3 * E2, CH * P], bf16)
        f2_bias = sb("f2_bias", [3 * E2, D], bf16)
        own = sb("own", [3 * E2, CH * P], fp32)
        part = sb("part", [3 * E2, CH * P], fp32)
        part2 = sb("part2", [3 * E2, CH * P], fp32)
        bpart = sb("bpart", [3 * E2, D], fp32)
        ident = sb("ident", [P, P], fp32)
        ident_h = sb("ident_h", [P, P], fp16)
        ident_b = sb("ident_b", [P, P], bf16)
        later = sb("later", [P, T], fp32)
        part_id = sb("part_id", [P, 1], fp32)
        t_row = sb("t_row", [B, T], fp32)
        rank8 = sb("rank8", [P, GS, E1], fp32)
        rank32 = sb("rank32", [P, GS, E2], fp32)
        e_base = sb("e_base", [P, GS * E1], fp32)
        neg_half = sb("neg_half", [P, GS], fp32)
        tok_i = sb("tok_i", [B, T], i32)
        tok_ci = sb("tok_ci", [P, B], i32)
        tok_c = sb("tok_c", [P, B], fp32)
        tok_z = sb("tok_z", [P, B], fp32)
        mask_r = sb("mask_r", [B, T], fp32)
        length = sb("length", [B, 1], fp32)
        pos_a = sb("pos_a", [B, T], fp32)
        pos_n = sb("pos_n", [B, T], fp32)
        pos_w = sb("pos_w", [B, T], fp32)
        pos_h = sb("pos_h", [B, T], bf16)
        tok_b = sb("tok_b", [P, B * T], i32)
        pos_b = sb("pos_b", [P, B * T], bf16)
        pos_dram = nc.dram_tensor("pos_scratch", [B, T], bf16, kind="Internal").ap()
        H = sb("H", [P, NG * GD], fp32)
        XS = sb("XS", [P, NG * GT], fp16)
        CW = sb("CW", [P, NG * GS * E1], fp32)
        onehot = sb("onehot", [P, GT], fp32)
        onehot129 = sb("onehot129", [1, GT], fp32)
        graph = sb("graph", [P, GS, T], fp32)
        peT = sb("peT", [D, GT], fp32)
        pe_sq = sb("pe_sq", [D, GT], fp32)
        pe_ss = sb("pe_ss", [D, GS], fp32)
        pe_sc = sb("pe_sc", [D, GS], fp32)
        pe_rn = sb("pe_rn", [D, GS], fp32)
        w_in_n = sb("w_in_n", [D, GS, D], fp32)
        hn = sb("hn", [P, GS, D + 1], fp32)
        deg = sb("deg", [P, GS], fp32)
        rdeg = sb("rdeg", [P, GS], fp32)
        gath = sb("gath", [P, GS, D], fp32)
        x1 = sb("x1", [P, GS, D], fp32)
        x1T = sb("x1T", [D, GT], fp32)
        state = sb("state", [P, GS, HALF], fp32)
        x2 = sb("x2", [P, GS, D], fp32)
        x2_parts = sb("x2_parts", [P, GS, 2, D], fp16)
        logit = sb("logit", [P, GS, E1], fp32)
        ldiff = sb("ldiff", [P, GS, E1], fp32)
        lexp = sb("lexp", [P, GS, E1], fp32)
        cand = sb("cand", [P, GS, E1], fp32)
        pick1 = sb("pick1", [P, GS, E1], fp32)
        rest = sb("rest", [P, GS, E1], fp32)
        cand2 = sb("cand2", [P, GS, E1], fp32)
        pick2 = sb("pick2", [P, GS, E1], fp32)
        lmax = sb("lmax", [P, 6, GS], fp32)
        cw_now = sb("cw_now", [P, GS * E1], fp32)
        cwT = sb("cwT", [GS * E1, P], fp32)
        hT = sb("hT", [P, 4, GT], fp32)
        prod = sb("prod", [P, 2, GS, 2, D], fp32)
        LN = ("rnn", "moe", "att", "ffn")
        bn = {k: sb(f"bn_{k}", [P, GS, 6], fp32) for k in LN}
        mv = {k: sb(f"mv_{k}", [P, GS, 2], fp32) for k in LN}
        ve = {k: sb(f"ve_{k}", [P, GS], fp32) for k in LN}
        rstd = {k: sb(f"rstd_{k}", [P, GS], fp32) for k in LN}
        x3 = sb("x3", [P, GS, D + 1], fp32)
        x3T = sb("x3T", [D, GT], fp32)
        expS = sb("expS", [P, GS, T], fp32)
        rden = sb("rden", [P, GS], fp32)
        ctxn = sb("ctxn", [P, GS, D], fp32)
        x4 = sb("x4", [P, GS, D], fp32)
        x4_parts = sb("x4_parts", [P, GS, 2, D], fp16)
        xs4 = sb("xs4", [P, GT], fp16)
        rlog = sb("rlog", [P, GS, E2], fp32)
        req = sb("req", [P, GS, E2], fp32)
        rmax = sb("rmax", [P, 2, GS], fp32)
        route = sb("route", [P, GS, 3, E2], bf16)
        routeT = sb("routeT", [3 * E2, GT], bf16)
        f1 = sb("f1", [P, CH, GT], fp32)

        ps_xp = bank("ps_xp")
        ps_t = bank("ps_t")
        ps_r = bank("ps_r")
        ps_up = [bank(f"ps_up{i}") for i in range(2)]
        ps_dn = [bank(f"ps_dn{i}") for i in range(2)]
        ps_x = bank("ps_x")
        ps_th = ps_t[:, 0:256].bitcast(fp16)
        ps_rh = ps_r[:, 0:256].bitcast(fp16)
        ps_rb = ps_r[:, 0:256].bitcast(bf16)

        w_ld, tok_ld, pos_st, grp_ld, out_st = (sem(n) for n in ("w_ld", "tok_ld", "pos_st", "grp_ld", "out_st"))
        consts, ids, prep, prep_a, pos_steps = (sem(n) for n in ("consts", "ids", "prep", "prep_a", "pos_steps"))
        onehot_rdy, graph_rdy, pe_mm, peT_rdy, sq_rdy, ss_rdy, pool_t, win_rdy = (sem(n) for n in (
            "onehot_rdy", "graph_rdy", "pe_mm", "peT_rdy", "sq_rdy", "ss_rdy", "pool_t", "win_rdy"))
        hn_mm, hn_rdy, gath_mm, gath_steps, h1_rdy = (sem(n) for n in (
            "hn_mm", "hn_rdy", "gath_mm", "gath_steps", "h1_rdy"))
        x1_rdy, x1T_mm, x1T_rdy, xp_mm, step_mm, state_rdy, back_mm = (sem(n) for n in (
            "x1_rdy", "x1T_mm", "x1T_rdy", "xp_mm", "step_mm", "state_rdy", "back_mm"))
        ln_bn = {k: sem(f"ln_bn_{k}") for k in LN}
        ln_mv = {k: sem(f"ln_mv_{k}") for k in LN}
        ln_ve = {k: sem(f"ln_ve_{k}") for k in LN}
        ln_rs = {k: sem(f"ln_rs_{k}") for k in LN}
        h2_rdy, x2_rdy, hi2_rdy, x2p_rdy, xsT_mm, xs_rdy, logit_mm, logit_rdy = (sem(n) for n in (
            "h2_rdy", "x2_rdy", "hi2_rdy", "x2p_rdy", "xsT_mm", "xs_rdy", "logit_mm", "logit_rdy"))
        ldiff_rdy, lexp_rdy, top_steps, cw_rdy, cwT_mm, cwT_rdy, b2_mm, h2b_rdy = (sem(n) for n in (
            "ldiff_rdy", "lexp_rdy", "top_steps", "cw_rdy", "cwT_mm", "cwT_rdy", "b2_mm", "h2b_rdy"))
        up_mm, gelu_rdy, dn_mm, prod_rdy, sum_a, sum_b = (sem(n) for n in (
            "up_mm", "gelu_rdy", "dn_mm", "prod_rdy", "sum_a", "sum_b"))
        x3_rdy, x3T_mm, x3T_rdy, s_mm, exp_rdy, ctx_mm, den_rdy, ctx_rdy, h4_rdy = (sem(n) for n in (
            "x3_rdy", "x3T_mm", "x3T_rdy", "s_mm", "exp_rdy", "ctx_mm", "den_rdy", "ctx_rdy", "h4_rdy"))
        x4_rdy, hi4_rdy, x4p_rdy, xs4T_mm, xs4_rdy, rlog_mm, rt_steps, route_rdy = (sem(n) for n in (
            "x4_rdy", "hi4_rdy", "x4p_rdy", "xs4T_mm", "xs4_rdy", "rlog_mm", "rt_steps", "route_rdy"))
        routeT_mm, routeT_rdy, f1_mm, f1_act, f1_dve, f2_mm, fin_rdy = (sem(n) for n in (
            "routeT_mm", "routeT_rdy", "f1_mm", "f1_act", "f1_dve", "f2_mm", "fin_rdy"))

        TOP_STEPS = 11
        RT_STEPS = 5

        def Hg(g):
            return H[:, bass.ts(g, GD)]

        def Hg3(g):
            return Hg(g).rearrange("p (s d) -> p s d", s=GS)

        def over_d(ap):
            return ap.unsqueeze(2).broadcast_to([ap.shape[0], GS, D])

        def over_e(ap, e):
            return ap.unsqueeze(2).broadcast_to([P, GS, e])

        def over_s(ap, rows, n):
            return ap.unsqueeze(1).broadcast_to([rows, GS, n])

        def wait_pos(eng, s, v):
            if not isinstance(v, int) or v > 0:
                eng.wait_ge(s, v)

        def hold(eng, s, v):
            eng.wait_ge(s, v)
            if not isinstance(v, int):
                eng.nop(nofuse=True)

        def run(program, lags):
            eng, body = program
            top = max(lags)

            def on(i):
                return [i - lag if 0 <= i - lag < NG else None for lag in lags]

            for i in range(top + 1):
                body(*on(i))
            with eng.Fori(top + 1, NG) as i:
                body(*[i - lag if lag else i for lag in lags])
            for i in range(NG, NG + top):
                body(*on(i))

        block = ctx.enter_context(nc.Block())

        @block.sync
        def _(sp):
            sp.dma_start(tok_i[:, :], tok).then_inc(tok_ld, 16)
            sp.dma_start(tok_ci[:, :], tok_cols).then_inc(tok_ld, 16)
            sp.dma_start(W[:, :], weights).then_inc(w_ld, 16)
            sp.dma_start(emb129[:, :], emb_last).then_inc(w_ld, 16)
            sp.dma_start(b2diag[:, :], diag_b2).then_inc(w_ld, 16)
            sp.wait_ge(pos_steps, 8)
            sp.dma_start(pos_dram, pos_h[:, :]).then_inc(pos_st, 16)
            sp.wait_ge(pos_st, 16)
            tok_flat = tok.rearrange("b t -> (b t)")
            pos_flat = pos_dram.rearrange("b t -> (b t)")

            def load_group(g):
                sp.dma_start(tok_b[:, bass.ts(g, GT)], tok_flat[bass.ts(g, GT)].partition_broadcast(P)).then_inc(grp_ld, 16)
                sp.dma_start(pos_b[:, bass.ts(g, GT)], pos_flat[bass.ts(g, GT)].partition_broadcast(P)).then_inc(grp_ld, 16)

            load_group(0)
            with sp.Fori(1, NG) as g:
                sp.wait_ge(grp_ld, g * 32)
                load_group(g)
            out_v = out.rearrange("b t d -> t b d")
            with sp.Fori(0, NG) as g:
                sp.wait_ge(fin_rdy, g + 1)
                sp.dma_start(out_v[:, bass.ts(g, GS), :], Hg3(g)).then_inc(out_st, 16)
            sp.wait_ge(out_st, 16 * NG)

        @block.gpsimd
        def _(pool):
            pool.memset(ident[:, :], 0.0)
            pool.memset(own[:, :], 0.0)
            pool.memset(later[:, :], 1.0)
            pool.memset(e_base[:, :], 2.718281828459045)
            pool.memset(neg_half[:, :], -0.5)
            pool.memset(whh_bd[:, :], 0.0)
            pool.memset(state[:, :, :], 0.0)
            pool.memset(hn[:, :, :], 1.0)
            pool.memset(x3[:, :, :], 1.0)
            pool.iota(t_row[:, :], [[1, T]], base=0, channel_multiplier=0, allow_small_or_imprecise_dtypes=True)
            pool.iota(part_id[:, :], [[0, 1]], base=0, channel_multiplier=1, allow_small_or_imprecise_dtypes=True)
            pool.iota(rank8[:, :, :], [[0, GS], [-1, E1]], base=E1, channel_multiplier=0, allow_small_or_imprecise_dtypes=True)
            pool.iota(rank32[:, :, :], [[0, GS], [-1, E2]], base=E2, channel_multiplier=0,
                      allow_small_or_imprecise_dtypes=True).then_inc(consts, 1)
            pool.wait_ge(consts, 1)
            pool.affine_select(out=ident[:, :], in_=ident[:, :], compare_op=ALU.not_equal, fill=1.0, base=0,
                               pattern=[[-1, P]], channel_multiplier=1)
            pool.affine_select(out=later[:, :], in_=later[:, :], compare_op=ALU.is_ge, fill=0.0, base=0,
                               pattern=[[-1, T]], channel_multiplier=1).then_inc(ids, 1)
            for k in range(3):
                pool.wait_ge(ids, k + 1)
                o = own[k * E2:(k + 1) * E2, :].rearrange("p (e h) -> p e h", h=H2)
                pool.affine_select(out=o, in_=o, compare_op=ALU.not_equal, fill=1.0, base=0,
                                   pattern=[[-1, E2], [0, H2]], channel_multiplier=1).then_inc(ids, 1)
            pool.wait_ge(ids, 4)
            pool.tensor_copy(ident_h[:, :], ident[:, :])
            pool.tensor_copy(ident_b[:, :], ident[:, :]).then_inc(ids, 1)

            def rstd_of(k, g):
                hold(pool, ln_mv[k], g + 1)
                pool.tensor_scalar(ve[k][:, :], mv[k][:, :, 1], EPS_LN, None, ALU.add).then_inc(ln_ve[k], 1)
                pool.wait_ge(ln_ve[k], g + 1)
                pool.tensor_tensor(rstd[k][:, :], ve[k][:, :], neg_half[:, :], ALU.pow).then_inc(ln_rs[k], 1)

            def body(t, n, r, m):
                if r is not None:
                    rstd_of("moe", r)
                if t is not None:
                    pool.wait_ge(peT_rdy, t + 1)
                    pool.tensor_tensor(pe_sq[:, :], peT[:, :], peT[:, :], ALU.mult).then_inc(sq_rdy, 1)
                    hold(pool, ss_rdy, t + 1)
                    pool.tensor_scalar(pe_sc[:, :], pe_ss[:, :], EPS_NORM_SQ, None, ALU.max).then_inc(pool_t, 1)
                    pool.wait_ge(pool_t, t * 2 + 1)
                    pool.tensor_tensor(pe_rn[:, :], pe_sc[:, :], neg_half[0:D, :], ALU.pow).then_inc(pool_t, 1)
                    pool.wait_ge(pool_t, t * 2 + 2)
                    pool.wait_ge(hn_mm, t)
                    pool.tensor_tensor(w_in_n[:, :, :], over_s(w("w_in")[0:D, :], D, D), over_d(pe_rn[:, :]),
                                       ALU.mult).then_inc(win_rdy, 1)
                if r is not None:
                    pool.wait_ge(ldiff_rdy, r + 1)
                    pool.tensor_tensor(lexp[:, :, :].rearrange("p s e -> p (s e)"), e_base[:, :],
                                       ldiff[:, :, :].rearrange("p s e -> p (s e)"), ALU.pow).then_inc(lexp_rdy, 1)

                def sums(p):
                    k = p % 2
                    if p:
                        pool.wait_ge(sum_b, m * 4 + p)
                    else:
                        pool.wait_ge(h2b_rdy, m + 1)
                    hold(pool, prod_rdy, m * 4 + (p + 1))
                    pool.tensor_tensor(Hg3(m), Hg3(m), prod[:, k, :, 0, :], ALU.add).then_inc(sum_a, 1)
                    hold(pool, sum_a, m * 4 + (p + 1))
                    pool.tensor_tensor(Hg3(m), Hg3(m), prod[:, k, :, 1, :], ALU.add).then_inc(sum_b, 1)

                if m is not None:
                    sums(0)
                    sums(1)
                if t is not None:
                    rstd_of("rnn", t)
                if m is not None:
                    sums(2)
                    sums(3)

            run((pool, body), (0, LAG_N, LAG_R, LAG_M))

            def tail(a, f):
                if a is not None:
                    rstd_of("att", a)
                if f is not None:
                    rstd_of("ffn", f)

            run((pool, tail), (0, 1))

        @block.scalar
        def _(act):
            def body(t, n, r, m):
                def gelu(e):
                    act.wait_ge(up_mm, m * 8 + (e + 1))
                    if not isinstance(m, int) or m * 8 + e - 3 > 0:
                        act.wait_ge(dn_mm, m * 8 + (e - 3))
                    act.activation(hT[:, e % 4, :], ps_up[e % 2][:, :], ACT.Gelu, bias=w("b1")[:, e:e + 1],
                                   scale=1.0 / WS).then_inc(gelu_rdy, 1)

                def tanh(k):
                    act.wait_ge(step_mm, n * 4 + (k + 1))
                    if k == 0:
                        wait_pos(act, back_mm, n)
                    act.activation(state[:, k, :], ps_xp[:, k * HALF:(k + 1) * HALF], ACT.Tanh,
                                   bias=rnn_bias[:, :]).then_inc(state_rdy, 1)

                if n is not None:
                    act.wait_ge(x1T_mm, n + 1)
                    wait_pos(act, xp_mm, n)
                    act.activation(x1T[:, :], ps_t[0:D, :], ACT.Copy).then_inc(x1T_rdy, 1)
                if m is not None:
                    gelu(0)
                    gelu(1)
                if n is not None:
                    tanh(0)
                if t is not None:
                    act.wait_ge(pe_mm, t + 1)
                    act.activation(peT[:, :], ps_t[0:D, :], ACT.Copy).then_inc(peT_rdy, 1)
                if r is not None:
                    act.wait_ge(xsT_mm, r + 1)
                    act.activation(XS[:, bass.ts(r, GT)], ps_rh, ACT.Copy).then_inc(xs_rdy, 1)
                if n is not None:
                    tanh(1)
                if m is not None:
                    gelu(2)
                if n is not None:
                    tanh(2)
                if m is not None:
                    gelu(3)
                if t is not None:
                    act.wait_ge(hn_mm, t + 1)
                    wait_pos(act, gath_mm, t)
                    act.activation(hn[:, :, 0:D], ps_t[:, 0:GD].rearrange("p (s d) -> p s d", s=GS),
                                   ACT.Copy).then_inc(hn_rdy, 1)
                if n is not None:
                    tanh(3)
                if m is not None:
                    gelu(4)
                    gelu(5)
                if r is not None:
                    act.wait_ge(cwT_mm, r + 1)
                    act.activation(cwT[:, :], ps_r[0:GS * E1, 0:P], ACT.Copy).then_inc(cwT_rdy, 1)
                if m is not None:
                    gelu(6)
                    gelu(7)

            act.wait_ge(prep, 1)
            run((act, body), (0, LAG_N, LAG_R, LAG_M))

            def tail(a, f):
                def relu(c):
                    act.wait_ge(f1_mm, f * 4 + (c + 1))
                    wait_pos(act, f2_mm, f)
                    act.activation(f1[:, c, :], ps_up[c % 2][:, :] if c < 2 else ps_dn[c % 2][:, :], ACT.Relu,
                                   scale=1.0 / WS).then_inc(f1_act, 1)

                if a is not None:
                    act.wait_ge(x3T_mm, a + 1)
                    act.activation(x3T[:, :], ps_t[0:D, :], ACT.Copy).then_inc(x3T_rdy, 1)
                if f is not None:
                    act.wait_ge(xs4T_mm, f + 1)
                    wait_pos(act, f1_mm, f * 4)
                    act.activation(xs4[:, :], ps_rh, ACT.Copy).then_inc(xs4_rdy, 1)
                if a is not None:
                    act.wait_ge(s_mm, a + 1)
                    wait_pos(act, ctx_mm, a)
                    act.activation(expS[:, :, :].rearrange("p s t -> p (s t)"), ps_t[:, :], ACT.Exp,
                                   scale=float(D) ** -0.5).then_inc(exp_rdy, 1)
                if f is not None:
                    act.wait_ge(routeT_mm, f + 1)
                    act.activation(routeT[:, :], ps_rb[0:3 * E2, :], ACT.Copy).then_inc(routeT_rdy, 1)
                    relu(0)
                    relu(2)

            run((act, tail), (0, 1))

        @block.tensor
        def _(pe):
            pe.wait_ge(ids, 5)
            pe.wait_ge(w_ld, 48)
            pe.wait_ge(prep, 1)

            def body(t, n, r, m):
                def up(e):
                    if not isinstance(m, int) or m * 8 + e - 1 > 0:
                        pe.wait_ge(gelu_rdy, m * 8 + (e - 1))
                    if e == 0:
                        pe.wait_ge(xs_rdy, m + 1)
                    xs = XS[:, bass.ts(m, GT)]
                    pe.matmul(ps_up[e % 2][:, :], w1_hi[:, e * H1:(e + 1) * H1], xs, start=True, stop=False)
                    pe.matmul(ps_up[e % 2][:, :], w1_lo[:, e * H1:(e + 1) * H1], xs, start=False,
                              stop=True).then_inc(up_mm, 1)

                def down(e):
                    pe.wait_ge(gelu_rdy, m * 8 + (e + 1))
                    p = e // 2
                    if e % 2 == 0 and (not isinstance(m, int) or m * 4 + p - 1 > 0):
                        pe.wait_ge(prod_rdy, m * 4 + (p - 1))
                    for s in range(GS):
                        c = s * 2 * D + (e % 2) * D
                        last = pe.matmul(ps_dn[p % 2][:, c:c + D], hT[:, e % 4, s * T:(s + 1) * T],
                                         w("w2")[:, e * D:(e + 1) * D], start=True, stop=True)
                    last.then_inc(dn_mm, 1)

                def step(k):
                    if k:
                        pe.wait_ge(state_rdy, n * 4 + k)
                    prev = (k - 1) % GS
                    pe.matmul(ps_xp[:, k * HALF:(k + 1) * HALF], whh_bd[:, :], state[:, prev, :], start=False,
                              stop=True, skip_group_check=True).then_inc(step_mm, 1)

                if n is not None:
                    hold(pe, x1_rdy, n + 1)
                    for s in range(GS):
                        last = pe.transpose(ps_t[0:D, s * T:(s + 1) * T], x1[:, s, :], ident[:, :])
                    last.then_inc(x1T_mm, 1)
                if m is not None:
                    up(0)
                    up(1)
                if n is not None:
                    pe.wait_ge(x1T_rdy, n + 1)
                    if not isinstance(n, int) or n > 0:
                        hold(pe, state_rdy, n * 4)
                    xin = x1T[:, :].rearrange("p (s c t) -> p c s t", s=GS, c=2)
                    for c in range(2):
                        last = pe.matmul(ps_xp[c * HALF:(c + 1) * HALF, 0:GS * HALF], w("w_ih")[0:D, :], xin[:, c],
                                         start=True, stop=False, skip_group_check=True)
                    last.then_inc(xp_mm, 1)
                    step(0)
                if t is not None:
                    pe.wait_ge(onehot_rdy, t + 1)
                    if n is not None:
                        pe.wait_ge(x1T_rdy, n + 1)
                    pe.matmul(ps_t[0:D, :], w("emb"), onehot[:, :], start=True, stop=False)
                    pe.matmul(ps_t[0:D, :], emb129[:, :], onehot129[:, :], start=False, stop=True).then_inc(pe_mm, 1)
                if m is not None:
                    down(0)
                if r is not None:
                    pe.wait_ge(x2p_rdy, r + 1)
                    for s in range(GS):
                        last = pe.transpose(ps_rh[:, s * T:(s + 1) * T],
                                            x2_parts[:, s, :, :].rearrange("p a d -> p (a d)"), ident_h[:, :])
                    last.then_inc(xsT_mm, 1)
                if n is not None:
                    step(1)
                if m is not None:
                    up(2)
                    down(1)
                if r is not None:
                    pe.wait_ge(xs_rdy, r + 1)
                    for s in range(GS):
                        x = XS[:, bass.ds(r * GT + s * T, T)]
                        pe.matmul(ps_r[:, s * E1:(s + 1) * E1], x, gate_hi[:, :], start=True, stop=False)
                        last = pe.matmul(ps_r[:, s * E1:(s + 1) * E1], x, gate_lo[:, :], start=False, stop=True)
                    last.then_inc(logit_mm, 1)
                if n is not None:
                    step(2)
                if m is not None:
                    up(3)
                    down(2)
                if t is not None:
                    pe.wait_ge(win_rdy, t + 1)
                    for s in range(GS):
                        last = pe.matmul(ps_t[:, s * D:(s + 1) * D], peT[:, s * T:(s + 1) * T], w_in_n[:, s, :],
                                         start=True, stop=True)
                    last.then_inc(hn_mm, 1)
                if n is not None:
                    step(3)
                if m is not None:
                    up(4)
                    down(3)
                    up(5)
                    down(4)
                if t is not None:
                    pe.wait_ge(graph_rdy, t + 1)
                    pe.wait_ge(hn_rdy, t + 1)
                    for s in range(GS):
                        last = pe.matmul(ps_t[:, s * (D + 1):(s + 1) * (D + 1)], graph[:, s, :], hn[:, s, :],
                                         start=True, stop=True)
                    last.then_inc(gath_mm, 1)
                if r is not None:
                    pe.wait_ge(cw_rdy, r + 1)
                    pe.transpose(ps_r[0:GS * E1, 0:P], cw_now[:, :],
                                 ident[:, :]).then_inc(cwT_mm, 1)
                if m is not None:
                    up(6)
                    down(5)
                if r is not None:
                    pe.wait_ge(cwT_rdy, r + 1)
                    pe.matmul(ps_r[:, 0:GD], cwT[:, :], b2diag[:, :], start=True, stop=True).then_inc(b2_mm, 1)
                if m is not None:
                    up(7)
                    down(6)
                if n is not None:
                    if r is not None:
                        pe.wait_ge(h2b_rdy, r + 1)
                    hold(pe, state_rdy, n * 4 + 4)
                    for k in range(GS):
                        for c in range(2):
                            h = slice(c * HALF, (c + 1) * HALF)
                            last = pe.matmul(ps_r[h, k * D:(k + 1) * D], state[h, k, :], ident[h, h],
                                             start=True, stop=True)
                    last.then_inc(back_mm, 1)
                if m is not None:
                    down(7)

            run((pe, body), (0, LAG_N, LAG_R, LAG_M))

            def tail(a, f):
                if a is not None:
                    wait_pos(pe, ctx_rdy, a)
                    hold(pe, x3_rdy, a + 1)
                    for s in range(GS):
                        last = pe.transpose(ps_t[0:D, s * T:(s + 1) * T], x3[:, s, 0:D], ident[:, :])
                    last.then_inc(x3T_mm, 1)
                if f is not None:
                    pe.wait_ge(x4p_rdy, f + 1)
                    for s in range(GS):
                        last = pe.transpose(ps_rh[:, s * T:(s + 1) * T],
                                            x4_parts[:, s, :, :].rearrange("p a d -> p (a d)"), ident_h[:, :])
                    last.then_inc(xs4T_mm, 1)
                if a is not None:
                    pe.wait_ge(x3T_rdy, a + 1)
                    for s in range(GS):
                        xt = x3T[:, s * T:(s + 1) * T]
                        last = pe.matmul(ps_t[:, s * T:(s + 1) * T], xt, xt, start=True, stop=True)
                    last.then_inc(s_mm, 1)
                if f is not None:
                    pe.wait_ge(xs4_rdy, f + 1)
                    for s in range(GS):
                        x = xs4[:, s * T:(s + 1) * T]
                        pe.matmul(ps_r[:, s * E2:(s + 1) * E2], x, rout_hi[:, :], start=True, stop=False)
                        last = pe.matmul(ps_r[:, s * E2:(s + 1) * E2], x, rout_lo[:, :], start=False, stop=True)
                    last.then_inc(rlog_mm, 1)
                if a is not None:
                    pe.wait_ge(exp_rdy, a + 1)
                    for s in range(GS):
                        last = pe.matmul(ps_t[:, s * (D + 1):(s + 1) * (D + 1)], expS[:, s, :], x3[:, s, :],
                                         start=True, stop=True)
                    last.then_inc(ctx_mm, 1)
                if f is not None:
                    pe.wait_ge(route_rdy, f + 1)
                    for s in range(GS):
                        last = pe.transpose(ps_rb[0:3 * E2, s * T:(s + 1) * T],
                                            route[:, s, :, :].rearrange("p a e -> p (a e)"), ident_b[:, :])
                    last.then_inc(routeT_mm, 1)
                    pe.wait_ge(routeT_rdy, f + 1)
                    for c in range(CH):
                        dst = (ps_up[c % 2] if c < 2 else ps_dn[c % 2])[:, :]
                        if c % 2 == 0:
                            wait_pos(pe, f1_act, f * 2 + c // 2 - 1 if c else f * 2 - 1)
                            wait_pos(pe, f1_act, f * 2)
                        else:
                            wait_pos(pe, f1_dve, f * 2)
                        cols = slice(c * P, (c + 1) * P)
                        pe.matmul(dst, f1_pick[:, cols], routeT[:, :], start=True, stop=False)
                        pe.matmul(dst, f1_hi[:, cols], xs4[:, :], start=False, stop=False)
                        pe.matmul(dst, f1_lo[:, cols], xs4[:, :], start=False, stop=True).then_inc(f1_mm, 1)
                    wait_pos(pe, fin_rdy, f)
                    for s in range(GS):
                        pe.matmul(ps_x[:, s * D:(s + 1) * D], routeT[:, s * T:(s + 1) * T], f2_bias[:, :],
                                  start=(s == 0), stop=False, skip_group_check=True)
                    for c in range(CH):
                        if c % 2 == 0:
                            pe.wait_ge(f1_act, f * 2 + (c // 2 + 1))
                        else:
                            pe.wait_ge(f1_dve, f * 2 + (c // 2 + 1))
                        for s in range(GS):
                            last = pe.matmul(ps_x[:, s * D:(s + 1) * D], f1[:, c, s * T:(s + 1) * T],
                                             w("f2")[:, c * D:(c + 1) * D], start=False, stop=(c == CH - 1),
                                             skip_group_check=True)
                    last.then_inc(f2_mm, 1)

            run((pe, tail), (0, 1))

        @block.vector
        def _(dve):
            steps = {"pos": 0, "prep": 0}

            def link(ins, s, key):
                steps[key] += 1
                ins.then_inc(s, 1)
                dve.wait_ge(s, steps[key])

            dve.wait_ge(tok_ld, 32)
            dve.wait_ge(consts, 1)
            link(dve.tensor_scalar(mask_r[:, :], tok_i[:, :], 0.0, None, ALU.not_equal), pos_steps, "pos")
            link(dve.reduce_sum(length[:, :], mask_r[:, :], AX.X), pos_steps, "pos")
            link(dve.tensor_scalar(pos_a[:, :], t_row[:, :], -1.0, length[:, :], ALU.mult, ALU.add), pos_steps, "pos")
            link(dve.tensor_scalar(pos_n[:, :], pos_a[:, :], 0.0, float(VROWS), ALU.is_lt, ALU.mult), pos_steps, "pos")
            link(dve.tensor_tensor(pos_w[:, :], pos_a[:, :], pos_n[:, :], ALU.add), pos_steps, "pos")
            link(dve.tensor_scalar(tok_z[:, :], tok_ci[:, :], 0.0, 0.5, ALU.is_equal, ALU.mult), pos_steps, "pos")
            link(dve.tensor_tensor(tok_c[:, :], tok_ci[:, :], tok_z[:, :], ALU.add), pos_steps, "pos")
            link(dve.tensor_tensor(pos_h[:, :], pos_w[:, :], mask_r[:, :], ALU.mult), pos_steps, "pos")
            dve.wait_ge(w_ld, 48)
            dve.wait_ge(ids, 5)
            for h in range(2):
                q = slice(h * HALF, (h + 1) * HALF)
                dve.tensor_copy(whh_bd[q, q], w("w_hh")[q, :])

            def halves(hi, lo, name):
                link(dve.tensor_scalar(w(name), w(name), WS, None, ALU.mult), prep_a, "prep")
                link(dve.tensor_copy(hi[:, :], w(name)), prep_a, "prep")
                link(dve.tensor_tensor(lo[:, :], w(name), hi[:, :], ALU.subtract), prep_a, "prep")

            halves(w1_hi, w1_lo, "w1")
            halves(gate_hi, gate_lo, "gate")
            halves(rout_hi, rout_lo, "rout")
            halves(f1_hi, f1_lo, "f1")
            q = [slice(k * E2, (k + 1) * E2) for k in range(3)]
            link(dve.scalar_tensor_tensor(out=part[:, :], in0=w("f1b")[0:3 * E2, :], scalar=WS, in1=own[:, :],
                                          op0=ALU.mult, op1=ALU.mult), prep_a, "prep")
            link(dve.tensor_scalar(own[0:E2, :], own[0:E2, :], -1.0, BIG, ALU.add, ALU.mult), prep_a, "prep")
            link(dve.tensor_copy(f1_pick[:, :], part[:, :]), prep_a, "prep")
            link(dve.tensor_tensor(part2[:, :], part[:, :], f1_pick[:, :], ALU.subtract), prep_a, "prep")
            link(dve.tensor_copy(f1_pick[q[1], :], part2[q[1], :]), prep_a, "prep")
            link(dve.tensor_copy(f1_pick[q[2], :], part2[q[2], :]), prep_a, "prep")
            link(dve.tensor_tensor(part[q[2], :], part2[q[2], :], f1_pick[q[2], :], ALU.subtract), prep_a, "prep")
            link(dve.tensor_copy(f1_pick[q[2], :], part[q[2], :]), prep_a, "prep")
            link(dve.tensor_tensor(f1_pick[q[0], :], f1_pick[q[0], :], own[q[0], :], ALU.add), prep_a, "prep")
            fb = w("f2b")[0:3 * E2, :]
            link(dve.tensor_copy(f2_bias[:, :], fb), prep_a, "prep")
            link(dve.tensor_tensor(bpart[:, :], fb, f2_bias[:, :], ALU.subtract), prep_a, "prep")
            link(dve.tensor_copy(f2_bias[q[1], :], bpart[q[1], :]), prep_a, "prep")
            link(dve.tensor_copy(f2_bias[q[2], :], bpart[q[2], :]), prep_a, "prep")
            link(dve.tensor_tensor(bpart[q[2], :], bpart[q[2], :], f2_bias[q[2], :], ALU.subtract), prep_a, "prep")
            link(dve.tensor_copy(f2_bias[q[2], :], bpart[q[2], :]), prep_a, "prep")
            dve.tensor_tensor(rnn_bias[:, :], w("b_ih"), w("b_hh"), ALU.add).then_inc(prep, 1)

            def stats_of(k, g, after=None):
                if after is not None:
                    hold(dve, after, g + 1)
                for s in range(GS):
                    last = dve.bn_stats(bn[k][:, s, :], Hg(g)[:, s * D:(s + 1) * D])
                last.then_inc(ln_bn[k], 1)
                hold(dve, ln_bn[k], g + 1)
                for s in range(GS):
                    last = dve.bn_aggr(mv[k][:, s, :], bn[k][:, s, :])
                last.then_inc(ln_mv[k], 1)

            def normalise(k, g, dst):
                dve.wait_ge(ln_rs[k], g + 1)
                for s in range(GS):
                    last = dve.tensor_scalar(dst[:, s, 0:D], Hg(g)[:, s * D:(s + 1) * D], mv[k][:, s, 0:1],
                                             rstd[k][:, s:s + 1], ALU.subtract, ALU.mult)
                return last

            def split(x, parts, g, hi_sem, x_sem):
                dve.wait_ge(x_sem, g + 1)
                dve.tensor_copy(parts[:, :, 0, :], x[:, :, :]).then_inc(hi_sem, 1)
                dve.wait_ge(hi_sem, g + 1)
                return dve.tensor_tensor(parts[:, :, 1, :], x[:, :, :], parts[:, :, 0, :], ALU.subtract)

            def body(t, n, r, m):
                def weigh(p):
                    dve.wait_ge(dn_mm, m * 8 + (2 * p + 2))
                    if not isinstance(m, int) or m * 4 + p - 1 > 0:
                        dve.wait_ge(sum_b, m * 4 + (p - 1))
                    cw = CW[:, bass.ts(m, GS * E1)].rearrange("p (s e) -> p s e", s=GS)[:, :, 2 * p:2 * p + 2]
                    dve.tensor_tensor(prod[:, p % 2, :, :, :],
                                      ps_dn[p % 2][:, :].rearrange("p (s k d) -> p s k d", s=GS, k=2),
                                      cw.unsqueeze(3).broadcast_to([P, GS, 2, D]), ALU.mult).then_inc(prod_rdy, 1)

                if r is not None:
                    dve.wait_ge(back_mm, r + 1)
                    dve.tensor_tensor(Hg(r), ps_r[:, 0:GD], Hg(r), ALU.add).then_inc(h2_rdy, 1)
                    stats_of("moe", r, h2_rdy)
                if t is not None:
                    dve.wait_ge(grp_ld, t * 32 + 32)
                    wait_pos(dve, pe_mm, t)
                    pos = pos_b[:, bass.ts(t, GT)]
                    dve.tensor_scalar(onehot[:, :], pos, part_id[:, :], None, ALU.is_equal)
                    dve.tensor_scalar(onehot129[:, :], pos_b[0:1, bass.ts(t, GT)], float(T), None,
                                      ALU.is_equal).then_inc(onehot_rdy, 1)
                if r is not None:
                    normalise("moe", r, x2).then_inc(x2_rdy, 1)
                    wait_pos(dve, xsT_mm, r)
                    split(x2, x2_parts, r, hi2_rdy, x2_rdy).then_inc(x2p_rdy, 1)
                if m is not None:
                    weigh(0)
                if t is not None:
                    dve.wait_ge(sq_rdy, t + 1)
                    dve.tensor_reduce(pe_ss[:, :], pe_sq[:, :].rearrange("p (s t) -> p s t", s=GS), AX.X,
                                      ALU.add).then_inc(ss_rdy, 1)
                    wait_pos(dve, gath_mm, t)
                    for s in range(GS):
                        last = dve.scalar_tensor_tensor(
                            out=graph[:, s, :], in0=tok_b[:, bass.ds(t * GT + s * T, T)],
                            scalar=tok_c[:, bass.ds(t * GS + s, 1)], in1=later[:, :], op0=ALU.is_equal, op1=ALU.mult)
                    last.then_inc(graph_rdy, 1)
                if r is not None:
                    route_top2(r)
                if m is not None:
                    weigh(1)
                if m is not None:
                    weigh(2)
                if t is not None:
                    sums = ps_t[:, 0:GS * (D + 1)].rearrange("p (s d) -> p s d", s=GS)
                    dve.wait_ge(gath_mm, t + 1)
                    dve.tensor_scalar(deg[:, :], sums[:, :, D], 1.0, None, ALU.max).then_inc(gath_steps, 1)
                    dve.wait_ge(gath_steps, t * 3 + 1)
                    dve.reciprocal(rdeg[:, :], deg[:, :]).then_inc(gath_steps, 1)
                    dve.wait_ge(gath_steps, t * 3 + 2)
                    dve.tensor_tensor(gath[:, :, :], sums[:, :, 0:D], over_d(rdeg[:, :]), ALU.mult).then_inc(gath_steps, 1)
                    dve.wait_ge(gath_steps, t * 3 + 3)
                    dve.tensor_tensor(Hg3(t), gath[:, :, :], over_s(w("b_oah"), P, D), ALU.add).then_inc(h1_rdy, 1)
                    stats_of("rnn", t, h1_rdy)
                if r is not None:
                    dve.wait_ge(b2_mm, r + 1)
                    dve.tensor_tensor(Hg(r), ps_r[:, 0:GD], Hg(r), ALU.add).then_inc(h2b_rdy, 1)
                if t is not None:
                    wait_pos(dve, x1T_mm, t)
                    normalise("rnn", t, x1).then_inc(x1_rdy, 1)
                if m is not None:
                    weigh(3)

            def route_top2(r):
                k = [0]

                def step(ins):
                    k[0] += 1
                    ins.then_inc(top_steps, 1)
                    dve.wait_ge(top_steps, r * TOP_STEPS + k[0])

                dve.wait_ge(logit_mm, r + 1)
                dve.scalar_tensor_tensor(out=logit[:, :, :], in0=ps_r[:, 0:GS * E1].rearrange("p (s e) -> p s e", s=GS),
                                         scalar=1.0 / WS, in1=over_s(w("gate_b"), P, E1), op0=ALU.mult,
                                         op1=ALU.add).then_inc(logit_rdy, 1)
                dve.wait_ge(logit_rdy, r + 1)
                step(dve.tensor_reduce(lmax[:, 0, :], logit[:, :, :], AX.X, ALU.max))
                dve.tensor_tensor(ldiff[:, :, :], logit[:, :, :], over_e(lmax[:, 0, :], E1),
                                  ALU.subtract).then_inc(ldiff_rdy, 1)
                dve.wait_ge(ldiff_rdy, r + 1)
                step(dve.scalar_tensor_tensor(out=cand[:, :, :], in0=ldiff[:, :, :], scalar=0.0, in1=rank8[:, :, :],
                                              op0=ALU.is_equal, op1=ALU.mult))
                step(dve.tensor_reduce(lmax[:, 1, :], cand[:, :, :], AX.X, ALU.max))
                step(dve.tensor_tensor(pick1[:, :, :], cand[:, :, :], over_e(lmax[:, 1, :], E1), ALU.is_equal))
                step(dve.scalar_tensor_tensor(out=rest[:, :, :], in0=pick1[:, :, :], scalar=-BIG, in1=ldiff[:, :, :],
                                              op0=ALU.mult, op1=ALU.add))
                step(dve.tensor_reduce(lmax[:, 2, :], rest[:, :, :], AX.X, ALU.max))
                step(dve.tensor_tensor(cand2[:, :, :], rest[:, :, :], over_e(lmax[:, 2, :], E1), ALU.is_equal))
                step(dve.tensor_tensor(cand2[:, :, :], cand2[:, :, :], rank8[:, :, :], ALU.mult))
                dve.tensor_reduce(lmax[:, 3, :], cand2[:, :, :], AX.X, ALU.max)
                dve.wait_ge(lexp_rdy, r + 1)
                step(dve.tensor_reduce(lmax[:, 4, :], lexp[:, :, :], AX.X, ALU.add))
                dve.reciprocal(lmax[:, 5, :], lmax[:, 4, :])
                step(dve.tensor_tensor(pick2[:, :, :], cand2[:, :, :], over_e(lmax[:, 3, :], E1), ALU.is_equal))
                dve.tensor_tensor(lexp[:, :, :], lexp[:, :, :], over_e(lmax[:, 5, :], E1), ALU.mult)
                step(dve.tensor_tensor(pick1[:, :, :], pick1[:, :, :], pick2[:, :, :], ALU.add))
                wait_pos(dve, cwT_mm, r)
                dve.tensor_tensor(cw_now[:, :].rearrange("p (s e) -> p s e", s=GS), lexp[:, :, :], pick1[:, :, :], ALU.mult)
                dve.tensor_tensor(CW[:, bass.ts(r, GS * E1)].rearrange("p (s e) -> p s e", s=GS), lexp[:, :, :],
                                  pick1[:, :, :], ALU.mult).then_inc(cw_rdy, 1)
                assert k[0] == TOP_STEPS

            run((dve, body), (0, LAG_N, LAG_R, LAG_M))

            def tail(a, f):
                if a is not None:
                    if isinstance(a, int) and a == 0:
                        dve.wait_ge(sum_b, 4 * NG)
                    stats_of("att", a)
                if f is not None:
                    stats_of("ffn", f, h4_rdy)
                if a is not None:
                    wait_pos(dve, ctx_mm, a)
                    normalise("att", a, x3).then_inc(x3_rdy, 1)
                if f is not None:
                    normalise("ffn", f, x4).then_inc(x4_rdy, 1)
                    split(x4, x4_parts, f, hi4_rdy, x4_rdy).then_inc(x4p_rdy, 1)
                    dve.wait_ge(rlog_mm, f + 1)
                    dve.scalar_tensor_tensor(out=rlog[:, :, :], in0=ps_r[:, 0:GS * E2].rearrange("p (s e) -> p s e", s=GS),
                                             scalar=1.0 / WS, in1=over_s(w("rout_b"), P, E2), op0=ALU.mult,
                                             op1=ALU.add).then_inc(rt_steps, 1)
                    dve.wait_ge(rt_steps, f * RT_STEPS + 1)
                    dve.tensor_reduce(rmax[:, 0, :], rlog[:, :, :], AX.X, ALU.max).then_inc(rt_steps, 1)
                    dve.wait_ge(rt_steps, f * RT_STEPS + 2)
                    dve.tensor_tensor(req[:, :, :], rlog[:, :, :], over_e(rmax[:, 0, :], E2),
                                      ALU.is_equal).then_inc(rt_steps, 1)
                    dve.wait_ge(rt_steps, f * RT_STEPS + 3)
                    dve.tensor_tensor(rlog[:, :, :], req[:, :, :], rank32[:, :, :], ALU.mult).then_inc(rt_steps, 1)
                    dve.wait_ge(rt_steps, f * RT_STEPS + 4)
                    dve.tensor_reduce(rmax[:, 1, :], rlog[:, :, :], AX.X, ALU.max).then_inc(rt_steps, 1)
                    dve.wait_ge(rt_steps, f * RT_STEPS + 5)
                    wait_pos(dve, routeT_mm, f)
                    for k in range(3):
                        last = dve.tensor_tensor(route[:, :, k, :], rlog[:, :, :], over_e(rmax[:, 1, :], E2), ALU.is_equal)
                    last.then_inc(route_rdy, 1)
                if a is not None:
                    sums = ps_t[:, 0:GS * (D + 1)].rearrange("p (s d) -> p s d", s=GS)
                    dve.wait_ge(ctx_mm, a + 1)
                    dve.reciprocal(rden[:, :], sums[:, :, D]).then_inc(den_rdy, 1)
                    dve.wait_ge(den_rdy, a + 1)
                    dve.tensor_tensor(ctxn[:, :, :], sums[:, :, 0:D], over_d(rden[:, :]), ALU.mult).then_inc(ctx_rdy, 1)
                    dve.wait_ge(ctx_rdy, a + 1)
                    dve.tensor_tensor(Hg3(a), ctxn[:, :, :], Hg3(a), ALU.add).then_inc(h4_rdy, 1)
                if f is not None:
                    for c in (1, 3):
                        dve.wait_ge(f1_mm, f * 4 + (c + 1))
                        dve.tensor_scalar(f1[:, c, :], (ps_up[1] if c < 2 else ps_dn[1])[:, :], 1.0 / WS, 0.0, ALU.mult,
                                          ALU.max).then_inc(f1_dve, 1)
                    dve.wait_ge(f2_mm, f + 1)
                    dve.scalar_tensor_tensor(out=Hg3(f), in0=ps_x[:, 0:GD].rearrange("p (s d) -> p s d", s=GS),
                                             scalar=0.0, in1=Hg3(f), op0=ALU.max, op1=ALU.add).then_inc(fin_rdy, 1)

            run((dve, tail), (0, 1))


def kernel(**inputs):
    import numpy as _np
    import concourse.bacc as _bacc
    from concourse import mybir as _mybir
    from concourse.bass_utils import run_bass_kernel_spmd as _run

    x = {k: _np.ascontiguousarray(v) for k, v in inputs.items()}
    P = 128
    up, down = x["L0_ffn_W1"], x["L0_ffn_W2"]
    f_up, f_down = x["L1_ffn_W1"], x["L1_ffn_W2"]

    def twice(a):
        return _np.concatenate([a, a], 0)

    def every(a):
        return _np.tile(a.reshape(1, -1), (P, 1))

    def four(a):
        return _np.tile(a, (4, 1))

    pieces = {
        "emb": x["L0_tok_emb_table"][:P],
        "w_in": twice(x["L0_tok_W_in"].T),
        "w_ih": twice(x["L0_attn_W_ih"].T),
        "w_hh": twice(x["L0_attn_W_hh"].T),
        "b_ih": twice(x["L0_attn_b_ih"].reshape(-1, 1)),
        "b_hh": twice(x["L0_attn_b_hh"].reshape(-1, 1)),
        "b_oah": every(x["L0_tok_b_oah"]),
        "w1": twice(up.transpose(1, 0, 2).reshape(64, -1)),
        "b1": x["L0_ffn_b1"].T,
        "w2": down.transpose(1, 0, 2).reshape(P, -1),
        "gate": twice(x["L0_ffn_gate_w"]),
        "gate_b": every(x["L0_ffn_gate_b"]),
        "rout": twice(x["L1_ffn_router_w"].T),
        "rout_b": every(x["L1_ffn_router_b"]),
        "f1": twice(f_up.transpose(1, 0, 2).reshape(64, -1)),
        "f1b": every(x["L1_ffn_b1"]),
        "f2": f_down.reshape(4, P, 64).transpose(1, 0, 2).reshape(P, -1),
        "f2b": four(x["L1_ffn_b2"]),
    }
    cols, at = {}, 0
    for name, piece in pieces.items():
        cols[name] = (at, piece.shape[1])
        at += piece.shape[1]
    cols["_total"] = at
    weights = _np.ascontiguousarray(_np.concatenate(list(pieces.values()), 1))
    b2 = x["L0_ffn_b2"]
    b2_diag = _np.zeros((32, 256), b2.dtype)
    for s in range(4):
        b2_diag[8 * s:8 * s + 8, 64 * s:64 * s + 64] = b2
    arrays = {
        "tok": x["x"],
        "tok_cols": _np.ascontiguousarray(x["x"].T),
        "weights": weights,
        "diag_b2": b2_diag,
        "emb_last": _np.ascontiguousarray(x["L0_tok_emb_table"][P:]),
    }
    nc = _bacc.Bacc("TRN2", target_bir_lowering=False, num_devices=1)
    args = [nc.dram_tensor(n, a.shape, _mybir.dt.from_np(a.dtype), kind="ExternalInput").ap() for n, a in arrays.items()]
    out = nc.dram_tensor("out", (64, 128, 64), _mybir.dt.float32, kind="ExternalOutput").ap()
    lm_tower_kernel(nc, *args, out, cols)
    r = _run(nc, [arrays], core_ids=[0])
    return r.results[0]["out"]
```

```python
import concourse.bass as bass
from concourse import mybir
from contextlib import ExitStack


def lm_tower_kernel(nc, tok, tok_cols, weights, emb_tail, out, COLS):
    fp32, bf16, fp16, i32 = (mybir.dt.float32, mybir.dt.bfloat16, mybir.dt.float16, mybir.dt.int32)
    ALU = mybir.AluOpType
    ACT = mybir.ActivationFunctionType
    AX = mybir.AxisListType

    P = 128
    B, T = tok.shape
    D = 64
    HALF = P // 2
    VROWS = T + 1
    GS = 4
    NG = B // GS
    GT = GS * T
    GD = GS * D
    E1, H1 = 8, 128
    E2, H2 = 32, 16
    CH = E2 * H2 // P
    WS = 256.0
    BIG = 2.0 ** 100
    EPS_LN = 1e-5
    EPS_NORM_SQ = 1e-24

    ctx = ExitStack()
    with ctx:
        def sb(name, shape, dt):
            return ctx.enter_context(nc.sbuf_tensor(name, shape, dt))

        def bank(name):
            return ctx.enter_context(nc.psum_tensor(name, [P, 512], fp32))

        def sem(name):
            return ctx.enter_context(nc.semaphore(name))

        W = sb("W", [P, COLS["_total"]], fp32)

        def w(name):
            a, n = COLS[name]
            return W[:, a:a + n]

        emb_last = sb("emb_last", [3 * 32, D], fp32)
        emb_p = sb("emb_p", [P, 3, D], bf16)
        emb_r = sb("emb_r", [P, D], fp32)
        emb_lp = sb("emb_lp", [3 * 32, D], bf16)
        emb_l = sb("emb_l", [3 * 32, D], bf16)
        b2_parts = sb("b2_parts", [3 * 32, E1 * D], bf16)
        b2_rest = sb("b2_rest", [3 * 32, E1 * D], fp32)
        ones3 = sb("ones3", [3 * 32, P], bf16)
        whh_bd = sb("whh_bd", [P, P], fp32)
        rnn_bias = sb("rnn_bias", [P, 1], fp32)
        w1_hi = sb("w1_hi", [P, E1 * H1], fp16)
        w1_lo = sb("w1_lo", [P, E1 * H1], fp16)
        gate_hi = sb("gate_hi", [P, E1], fp16)
        gate_lo = sb("gate_lo", [P, E1], fp16)
        rout_hi = sb("rout_hi", [P, E2], fp16)
        rout_lo = sb("rout_lo", [P, E2], fp16)
        f1_hi = sb("f1_hi", [P, CH * P], fp16)
        f1_lo = sb("f1_lo", [P, CH * P], fp16)
        f1_pick = sb("f1_pick", [3 * E2, CH * P], bf16)
        f2_bias = sb("f2_bias", [3 * E2, D], bf16)
        own = sb("own", [3 * E2, CH * P], fp32)
        part = sb("part", [3 * E2, CH * P], fp32)
        part2 = sb("part2", [3 * E2, CH * P], fp32)
        bpart = sb("bpart", [3 * E2, D], fp32)
        ident = sb("ident", [P, P], fp32)
        ident_h = sb("ident_h", [P, P], fp16)
        ident_b = sb("ident_b", [P, P], bf16)
        later = sb("later", [P, T], fp32)
        part_id = sb("part_id", [P, 1], fp32)
        t_row = sb("t_row", [B, T], fp32)
        rank8 = sb("rank8", [P, GS, E1], fp32)
        rank32 = sb("rank32", [P, GS, E2], fp32)
        neg_half = sb("neg_half", [P, GS], fp32)
        tok_i = sb("tok_i", [B, T], i32)
        tok_ci = sb("tok_ci", [P, B], i32)
        tok_c = sb("tok_c", [P, B], fp32)
        tok_z = sb("tok_z", [P, B], fp32)
        mask_r = sb("mask_r", [B, T], fp32)
        length = sb("length", [B, 1], fp32)
        pos_a = sb("pos_a", [B, T], fp32)
        pos_n = sb("pos_n", [B, T], fp32)
        pos_w = sb("pos_w", [B, T], fp32)
        pos_h = sb("pos_h", [B, T], bf16)
        tok_b = sb("tok_b", [P, B * T], i32)
        pos_b = sb("pos_b", [P, B * T], bf16)
        pos_dram = nc.dram_tensor("pos_scratch", [B, T], bf16, kind="Internal").ap()
        H = sb("H", [P, NG * GD], fp32)
        XS = sb("XS", [P, NG * GT], fp16)
        CW = sb("CW", [P, NG * GS * E1], fp32)
        onehot = sb("onehot", [P, GT], bf16)
        onehot_l = sb("onehot_l", [3 * 32, GT], bf16)
        graph = sb("graph", [P, GS, T], fp32)
        peT = sb("peT", [D, GT], fp32)
        pe_sq = sb("pe_sq", [D, GT], fp32)
        pe_ss = sb("pe_ss", [D, GS], fp32)
        pe_sc = sb("pe_sc", [D, GS], fp32)
        pe_rn = sb("pe_rn", [D, GS], fp32)
        w_in_n = sb("w_in_n", [D, GS, D], fp32)
        hn = sb("hn", [P, GS, D + 1], fp32)
        deg = sb("deg", [P, GS], fp32)
        rdeg = sb("rdeg", [P, GS], fp32)
        x1 = sb("x1", [P, GS, D], fp32)
        x1T = sb("x1T", [D, GT], fp32)
        state = sb("state", [P, GS, HALF], fp32)
        x2 = sb("x2", [P, GS, D], fp32)
        x2_parts = sb("x2_parts", [P, GS, 2, D], fp16)
        logit = sb("logit", [P, GS, E1], fp32)
        ldiff = sb("ldiff", [P, GS, E1], fp32)
        lexp = sb("lexp", [P, GS, E1], fp32)
        cand = sb("cand", [P, GS, E1], fp32)
        pick1 = sb("pick1", [P, GS, E1], fp32)
        rest = sb("rest", [P, GS, E1], fp32)
        cand2 = sb("cand2", [P, GS, E1], fp32)
        pick2 = sb("pick2", [P, GS, E1], fp32)
        rank2 = sb("rank2", [P, GS, E1], fp32)
        picks = sb("picks", [P, GS, E1], fp32)
        lrec = sb("lrec", [P, GS, E1], fp32)
        lpick = sb("lpick", [P, GS, E1], fp32)
        lmax = sb("lmax", [P, 6, GS], fp32)
        lth = sb("lth", [P, GS, E1], fp32)
        lden = sb("lden", [P, GS, E1], fp32)
        lroot = sb("lroot", [P, 2, GS, E1], fp32)
        hT = sb("hT", [P, 4, GT], fp32)
        prod = sb("prod", [P, 2, GS, 2, D], fp32)
        LN = ("rnn", "moe", "att", "ffn")
        bn = {k: sb(f"bn_{k}", [P, GS, 6], fp32) for k in LN}
        mv = {k: sb(f"mv_{k}", [P, GS, 2], fp32) for k in LN}
        ve = {k: sb(f"ve_{k}", [P, GS], fp32) for k in LN}
        nm = {k: sb(f"nm_{k}", [P, GS], fp32) for k in LN}
        nmr = {k: sb(f"nmr_{k}", [P, GS], fp32) for k in LN}
        rstd = {k: sb(f"rstd_{k}", [P, GS], fp32) for k in LN}
        x3 = sb("x3", [P, GS, D + 1], fp32)
        x3T = sb("x3T", [D, GT], fp32)
        expS = sb("expS", [P, GS, T], fp32)
        rden = sb("rden", [P, GS], fp32)
        ctxn = sb("ctxn", [P, GS, D], fp32)
        x4_s = sb("x4_s", [P, GS, D], fp32)
        x4 = sb("x4", [P, GS, D], fp32)
        x4_parts = sb("x4_parts", [P, GS, 2, D], fp16)
        rlog = sb("rlog", [P, GS, E2], fp32)
        req = sb("req", [P, GS, E2], fp32)
        rrank = sb("rrank", [P, GS, E2], fp32)
        rmax = sb("rmax", [P, 2, GS], fp32)
        route = sb("route", [P, GS, 3, E2], bf16)
        RT = sb("RT", [3 * E2, NG * GT], bf16)
        f1 = sb("f1", [P, CH, GT], fp32)

        ps_xp = bank("ps_xp")
        ps_t = bank("ps_t")
        ps_r = bank("ps_r")
        ps_up = [bank(f"ps_up{i}") for i in range(2)]
        ps_dn = [bank(f"ps_dn{i}") for i in range(2)]
        ps_x = bank("ps_x")
        ps_f1 = [ps_up[0], ps_up[1], ps_dn[0], ps_dn[1]]
        ps_rh = ps_r[:, 0:256].bitcast(fp16)
        ps_xb = ps_xp[:, 0:256].bitcast(bf16)

        w_ld, tok_ld, pos_st, grp_ld, out_st = (sem(n) for n in ("w_ld", "tok_ld", "pos_st", "grp_ld", "out_st"))
        consts, ids, prep, prep_a, pos_steps = (sem(n) for n in ("consts", "ids", "prep", "prep_a", "pos_steps"))
        onehot_rdy, graph_rdy, pe_mm, peT_rdy, ss_rdy, pool_t, win_rdy = (sem(n) for n in (
            "onehot_rdy", "graph_rdy", "pe_mm", "peT_rdy", "ss_rdy", "pool_t", "win_rdy"))
        hn_mm, hn_rdy, gath_mm, deg_rdy, rdeg_rdy, h1_rdy = (sem(n) for n in (
            "hn_mm", "hn_rdy", "gath_mm", "deg_rdy", "rdeg_rdy", "h1_rdy"))
        x1_rdy, x1T_mm, x1T_rdy, xp_mm, step_mm, state_rdy, back_mm = (sem(n) for n in (
            "x1_rdy", "x1T_mm", "x1T_rdy", "xp_mm", "step_mm", "state_rdy", "back_mm"))
        ln_bn = {k: sem(f"ln_bn_{k}") for k in LN}
        ln_mv = {k: sem(f"ln_mv_{k}") for k in LN}
        ln_ve = {k: sem(f"ln_ve_{k}") for k in LN}
        ln_pw = {k: sem(f"ln_pw_{k}") for k in LN}
        ln_rs = {k: sem(f"ln_rs_{k}") for k in LN}
        h2_rdy, x2_rdy, hi2_rdy, x2p_rdy, xsT_mm, xs_rdy, logit_mm, logit_rdy = (sem(n) for n in (
            "h2_rdy", "x2_rdy", "hi2_rdy", "x2p_rdy", "xsT_mm", "xs_rdy", "logit_mm", "logit_rdy"))
        ldiff_rdy, lth_rdy, top_steps, sm_steps = (sem(n) for n in ("ldiff_rdy", "lth_rdy", "top_steps", "sm_steps"))
        up_mm, gelu_rdy, dn_mm, prod_rdy, sum_a, sum_b = (sem(n) for n in (
            "up_mm", "gelu_rdy", "dn_mm", "prod_rdy", "sum_a", "sum_b"))
        x3_rdy, x3T_mm, x3T_rdy, s_mm, exp_rdy, ctx_mm, den_rdy, ctx_rdy, h4_rdy = (sem(n) for n in (
            "x3_rdy", "x3T_mm", "x3T_rdy", "s_mm", "exp_rdy", "ctx_mm", "den_rdy", "ctx_rdy", "h4_rdy"))
        x4_scaled, x4_rdy, hi4_rdy, x4p_rdy, xs4T_mm, xs4_rdy, rlog_mm, rlog_rdy, rt_steps, route_rdy = (sem(n) for n in (
            "x4_scaled", "x4_rdy", "hi4_rdy", "x4p_rdy", "xs4T_mm", "xs4_rdy", "rlog_mm", "rlog_rdy", "rt_steps", "route_rdy"))
        routeT_mm, routeT_rdy, f1_mm, f1_act, f2_mm, fin_rdy = (sem(n) for n in (
            "routeT_mm", "routeT_rdy", "f1_mm", "f1_act", "f2_mm", "fin_rdy"))

        TOP_STEPS, SM_STEPS, RT_STEPS = 11, 9, 4

        def Hg(g):
            return H[:, bass.ts(g, GD)]

        def Hg3(g):
            return Hg(g).rearrange("p (s d) -> p s d", s=GS)

        def over_d(ap):
            return ap.unsqueeze(2).broadcast_to([ap.shape[0], GS, D])

        def over_e(ap, e):
            return ap.unsqueeze(2).broadcast_to([P, GS, e])

        def over_s(ap, rows, n):
            return ap.unsqueeze(1).broadcast_to([rows, GS, n])

        def wait_pos(eng, s, v):
            if not isinstance(v, int) or v > 0:
                eng.wait_ge(s, v)

        def hold(eng, s, v):
            eng.wait_ge(s, v)
            if not isinstance(v, int):
                eng.nop(nofuse=True)

        def run(eng, round_, top):
            for i in range(top + 1):
                round_(i)
            with eng.Fori(top + 1, NG) as i:
                round_(i)
            for i in range(NG, NG + top):
                round_(i)

        def step(work, g, *args):
            if not isinstance(g, int) or 0 <= g < NG:
                work(g, *args)

        def after_first(g):
            return not isinstance(g, int) or g > 0
        block = ctx.enter_context(nc.Block())

        @block.sync
        def _(sp):
            sp.dma_start(tok_i[:, :], tok).then_inc(tok_ld, 16)
            sp.dma_start(tok_ci[:, :], tok_cols).then_inc(tok_ld, 16)
            sp.dma_start(W[:, :], weights).then_inc(w_ld, 16)
            sp.dma_start(emb_last[:, :], emb_tail).then_inc(w_ld, 16)
            sp.wait_ge(pos_steps, 8)
            sp.dma_start(pos_dram, pos_h[:, :]).then_inc(pos_st, 16)
            sp.wait_ge(pos_st, 16)
            tok_flat = tok.rearrange("b t -> (b t)")
            pos_flat = pos_dram.rearrange("b t -> (b t)")

            def load_group(g):
                sp.dma_start(tok_b[:, bass.ts(g, GT)], tok_flat[bass.ts(g, GT)].partition_broadcast(P)).then_inc(grp_ld, 16)
                sp.dma_start(pos_b[:, bass.ts(g, GT)], pos_flat[bass.ts(g, GT)].partition_broadcast(P)).then_inc(grp_ld, 16)

            load_group(0)
            with sp.Fori(1, NG) as g:
                sp.wait_ge(grp_ld, g * 32)
                load_group(g)
            out_v = out.rearrange("b t d -> t b d")
            with sp.Fori(0, NG) as g:
                sp.wait_ge(fin_rdy, g + 1)
                sp.dma_start(out_v[:, bass.ts(g, GS), :], Hg3(g)).then_inc(out_st, 16)
            sp.wait_ge(out_st, 16 * NG)

        @block.gpsimd
        def _(pool):
            pool.memset(ident[:, :], 0.0)
            pool.memset(own[:, :], 0.0)
            pool.memset(later[:, :], 1.0)
            pool.memset(ones3[:, :], 0.0)
            pool.memset(emb_l[:, :], 0.0)
            pool.memset(neg_half[:, :], -0.5)
            pool.memset(whh_bd[:, :], 0.0)
            pool.memset(state[:, :, :], 0.0)
            pool.memset(hn[:, :, :], 1.0)
            pool.memset(x3[:, :, :], 1.0)
            pool.iota(t_row[:, :], [[1, T]], base=0, channel_multiplier=0, allow_small_or_imprecise_dtypes=True)
            pool.iota(part_id[:, :], [[0, 1]], base=0, channel_multiplier=1, allow_small_or_imprecise_dtypes=True)
            pool.iota(rank8[:, :, :], [[0, GS], [-1, E1]], base=E1, channel_multiplier=0, allow_small_or_imprecise_dtypes=True)
            pool.iota(rank32[:, :, :], [[0, GS], [-1, E2]], base=E2, channel_multiplier=0,
                      allow_small_or_imprecise_dtypes=True).then_inc(consts, 1)
            pool.wait_ge(consts, 1)
            pool.affine_select(out=ident[:, :], in_=ident[:, :], compare_op=ALU.not_equal, fill=1.0, base=0,
                               pattern=[[-1, P]], channel_multiplier=1)
            pool.affine_select(out=later[:, :], in_=later[:, :], compare_op=ALU.is_ge, fill=0.0, base=0,
                               pattern=[[-1, T]], channel_multiplier=1).then_inc(ids, 1)
            for k in range(3):
                pool.wait_ge(ids, k + 1)
                o = own[k * E2:(k + 1) * E2, :].rearrange("p (e h) -> p e h", h=H2)
                pool.affine_select(out=o, in_=o, compare_op=ALU.not_equal, fill=1.0, base=0,
                                   pattern=[[-1, E2], [0, H2]], channel_multiplier=1).then_inc(ids, 1)
            pool.wait_ge(ids, 4)
            pool.tensor_copy(ident_h[:, :], ident[:, :])
            pool.tensor_copy(ident_b[:, :], ident[:, :]).then_inc(ids, 1)

            def rstd_of(g, k, used):
                wait_pos(pool, ln_rs[k], g)
                hold(pool, ln_mv[k], g + 1)
                pool.tensor_scalar(ve[k][:, :], mv[k][:, :, 1], EPS_LN, None, ALU.add)
                pool.tensor_scalar(nm[k][:, :], mv[k][:, :, 0], -1.0, None, ALU.mult).then_inc(ln_ve[k], 1)
                wait_pos(pool, used, g)
                pool.wait_ge(ln_ve[k], g + 1)
                pool.tensor_tensor(rstd[k][:, :], ve[k][:, :], neg_half[:, :], ALU.pow).then_inc(ln_pw[k], 1)
                pool.wait_ge(ln_pw[k], g + 1)
                pool.tensor_tensor(nmr[k][:, :], nm[k][:, :], rstd[k][:, :], ALU.mult).then_inc(ln_rs[k], 1)

            def expert_sum(m, p):
                k = p % 2
                if after_first(m) or p > 0:
                    pool.wait_ge(sum_b, m * 4 + p)
                hold(pool, prod_rdy, m * 4 + (p + 1))
                pool.tensor_tensor(Hg3(m), Hg3(m), prod[:, k, :, 0, :], ALU.add).then_inc(sum_a, 1)
                hold(pool, sum_a, m * 4 + (p + 1))
                pool.tensor_tensor(Hg3(m), Hg3(m), prod[:, k, :, 1, :], ALU.add).then_inc(sum_b, 1)

            def scale_w_in(t):
                hold(pool, ss_rdy, t + 1)
                pool.tensor_scalar(pe_sc[:, :], pe_ss[:, :], EPS_NORM_SQ, None, ALU.max).then_inc(pool_t, 1)
                pool.wait_ge(pool_t, t * 2 + 1)
                pool.tensor_tensor(pe_rn[:, :], pe_sc[:, :], neg_half[0:D, :], ALU.pow).then_inc(pool_t, 1)
                pool.wait_ge(pool_t, t * 2 + 2)
                wait_pos(pool, hn_mm, t)
                pool.tensor_tensor(w_in_n[:, :, :], over_s(w("w_in")[0:D, :], D, D), over_d(pe_rn[:, :]),
                                   ALU.mult).then_inc(win_rdy, 1)

            def front(i):
                step(rstd_of, i - 3, "moe", x2_rdy)
                step(expert_sum, i - 5, 2)
                step(rstd_of, i - 1, "rnn", x1_rdy)
                step(expert_sum, i - 5, 3)
                step(scale_w_in, i)
                step(expert_sum, i - 4, 0)
                step(expert_sum, i - 4, 1)

            run(pool, front, 5)

            def add_context(a):
                hold(pool, ctx_rdy, a + 1)
                pool.tensor_tensor(Hg3(a), Hg3(a), ctxn[:, :, :], ALU.add).then_inc(h4_rdy, 1)

            def normalise_ffn(f):
                wait_pos(pool, x4p_rdy, f)
                hold(pool, ln_rs["ffn"], f + 1)
                pool.tensor_tensor(x4_s[:, :, :], Hg3(f), over_d(rstd["ffn"][:, :]), ALU.mult).then_inc(x4_scaled, 1)
                hold(pool, x4_scaled, f + 1)
                pool.tensor_tensor(x4[:, :, :], x4_s[:, :, :], over_d(nmr["ffn"][:, :]), ALU.add).then_inc(x4_rdy, 1)

            def back(i):
                step(rstd_of, i, "att", x3_rdy)
                step(rstd_of, i - 2, "ffn", x4_rdy)
                step(normalise_ffn, i - 2)
                step(add_context, i - 1)

            run(pool, back, 2)

        @block.scalar
        def _(act):
            def normalise(g, k, dst, free, done):
                wait_pos(act, free, g)
                act.wait_ge(ln_rs[k], g + 1)
                for s in range(GS):
                    last = act.activation(dst[:, s, 0:D], Hg(g)[:, s * D:(s + 1) * D], ACT.Identity,
                                          bias=nmr[k][:, s:s + 1], scale=rstd[k][:, s:s + 1])
                last.then_inc(done, 1)

            def pe_squares(t):
                act.wait_ge(pe_mm, t + 1)
                wait_pos(act, win_rdy, t)
                for s in range(GS):
                    last = act.activation(pe_sq[:, s * T:(s + 1) * T], ps_t[0:D, s * T:(s + 1) * T], ACT.Square,
                                          accum_out=pe_ss[:, s:s + 1])
                last.then_inc(ss_rdy, 1)

            def pe_out(t):
                act.wait_ge(pe_mm, t + 1)
                wait_pos(act, hn_mm, t)
                act.activation(peT[:, :], ps_t[0:D, :], ACT.Copy).then_inc(peT_rdy, 1)

            def hn_out(t):
                act.wait_ge(hn_mm, t + 1)
                wait_pos(act, gath_mm, t)
                act.activation(hn[:, :, 0:D], ps_t[:, 0:GD].rearrange("p (s d) -> p s d", s=GS),
                               ACT.Copy).then_inc(hn_rdy, 1)

            def x1T_out(n):
                act.wait_ge(x1T_mm, n + 1)
                wait_pos(act, xp_mm, n)
                act.activation(x1T[:, :], ps_x[0:D, :], ACT.Copy).then_inc(x1T_rdy, 1)

            def tanh(n, k):
                act.wait_ge(step_mm, n * 4 + (k + 1))
                if k == 0:
                    wait_pos(act, back_mm, n)
                act.activation(state[:, k, :], ps_xp[:, k * HALF:(k + 1) * HALF], ACT.Tanh,
                               bias=rnn_bias[:, :]).then_inc(state_rdy, 1)

            def xs_out(r):
                act.wait_ge(xsT_mm, r + 1)
                act.activation(XS[:, bass.ts(r, GT)], ps_rh, ACT.Copy).then_inc(xs_rdy, 1)

            def logit_tanh(r):
                act.wait_ge(ldiff_rdy, r + 1)
                act.activation(lth[:, :, :], ldiff[:, :, :], ACT.Tanh, scale=1.0 / 8).then_inc(lth_rdy, 1)

            def gelu(m, e):
                act.wait_ge(up_mm, m * 8 + (e + 1))
                if after_first(m) or e > 3:
                    act.wait_ge(dn_mm, m * 8 + (e - 3))
                act.activation(hT[:, e % 4, :], ps_up[e % 2][:, :], ACT.Gelu, bias=w("b1")[:, e:e + 1],
                               scale=1.0 / WS).then_inc(gelu_rdy, 1)

            def front(i):
                step(logit_tanh, i - 4)
                step(hn_out, i - 1)
                step(gelu, i - 4, 0)
                step(x1T_out, i - 2)
                step(gelu, i - 4, 1)
                step(gelu, i - 4, 2)
                step(tanh, i - 2, 0)
                step(normalise, i - 3, "moe", x2, x2p_rdy, x2_rdy)
                step(gelu, i - 4, 3)
                step(tanh, i - 2, 1)
                step(gelu, i - 4, 4)
                step(pe_squares, i)
                step(tanh, i - 2, 2)
                step(xs_out, i - 3)
                step(gelu, i - 4, 5)
                step(pe_out, i)
                step(tanh, i - 2, 3)
                step(gelu, i - 4, 6)
                step(normalise, i - 1, "rnn", x1, x1T_mm, x1_rdy)
                step(gelu, i - 4, 7)

            act.wait_ge(prep, 1)
            run(act, front, 4)

            def x3T_out(a):
                act.wait_ge(x3T_mm, a + 1)
                wait_pos(act, s_mm, a)
                act.activation(x3T[:, :], ps_t[0:D, :], ACT.Copy).then_inc(x3T_rdy, 1)

            def exp(a):
                act.wait_ge(s_mm, a + 1)
                wait_pos(act, ctx_mm, a)
                act.activation(expS[:, :, :].rearrange("p s t -> p (s t)"), ps_t[:, :], ACT.Exp,
                               scale=float(D) ** -0.5).then_inc(exp_rdy, 1)

            def xs4_out(f):
                act.wait_ge(xs4T_mm, f + 1)
                act.activation(XS[:, bass.ts(f, GT)], ps_rh, ACT.Copy).then_inc(xs4_rdy, 1)

            def route_out(f):
                act.wait_ge(routeT_mm, f + 1)
                act.activation(RT[:, bass.ts(f, GT)], ps_xb[0:3 * E2, :], ACT.Copy).then_inc(routeT_rdy, 1)

            def relu(f, c):
                act.wait_ge(f1_mm, f * 4 + (c + 1))
                wait_pos(act, f2_mm, f)
                act.activation(f1[:, c, :], ps_f1[c][:, :], ACT.Relu, scale=1.0 / WS).then_inc(f1_act, 1)

            def back(i):
                step(xs4_out, i - 3)
                step(exp, i - 1)
                step(relu, i - 4, 0)
                step(relu, i - 4, 1)
                step(normalise, i, "att", x3, ctx_mm, x3_rdy)
                step(relu, i - 4, 2)
                step(relu, i - 4, 3)
                step(route_out, i - 3)
                step(x3T_out, i)

            run(act, back, 4)

        @block.tensor
        def _(pe):
            pe.wait_ge(ids, 5)
            pe.wait_ge(w_ld, 32)
            pe.wait_ge(prep, 1)

            def embed(t):
                wait_pos(pe, h1_rdy, t)
                pe.wait_ge(onehot_rdy, t + 1)
                for k in range(3):
                    pe.matmul(ps_t[0:D, :], emb_p[:, k, :], onehot[:, :], start=(k == 0), stop=False)
                pe.matmul(ps_t[0:D, :], emb_l[:, :], onehot_l[:, :], start=False, stop=True).then_inc(pe_mm, 1)

            def project(t):
                pe.wait_ge(win_rdy, t + 1)
                pe.wait_ge(peT_rdy, t + 1)
                for s in range(GS):
                    last = pe.matmul(ps_t[:, s * D:(s + 1) * D], peT[:, s * T:(s + 1) * T], w_in_n[:, s, :],
                                     start=True, stop=True)
                last.then_inc(hn_mm, 1)

            def gather(t):
                pe.wait_ge(graph_rdy, t + 1)
                pe.wait_ge(hn_rdy, t + 1)
                for s in range(GS):
                    last = pe.matmul(ps_t[:, s * (D + 1):(s + 1) * (D + 1)], graph[:, s, :], hn[:, s, :],
                                     start=True, stop=True)
                last.then_inc(gath_mm, 1)

            def turn_x1(n):
                wait_pos(pe, x1T_rdy, n)
                hold(pe, x1_rdy, n + 1)
                for s in range(GS):
                    last = pe.transpose(ps_x[0:D, s * T:(s + 1) * T], x1[:, s, :], ident[:, :])
                last.then_inc(x1T_mm, 1)

            def rnn_step(n, k):
                if k:
                    pe.wait_ge(state_rdy, n * 4 + k)
                prev = (k - 1) % GS
                pe.matmul(ps_xp[:, k * HALF:(k + 1) * HALF], whh_bd[:, :], state[:, prev, :], start=False,
                          stop=True, skip_group_check=True).then_inc(step_mm, 1)

            def rnn_input(n):
                pe.wait_ge(x1T_rdy, n + 1)
                if after_first(n):
                    hold(pe, state_rdy, n * 4)
                xin = x1T[:, :].rearrange("p (s c t) -> p c s t", s=GS, c=2)
                for c in range(2):
                    last = pe.matmul(ps_xp[c * HALF:(c + 1) * HALF, 0:GS * HALF], w("w_ih")[0:D, :], xin[:, c],
                                     start=True, stop=False, skip_group_check=True)
                last.then_inc(xp_mm, 1)
                rnn_step(n, 0)

            def states_back(n):
                wait_pos(pe, logit_rdy, n)
                hold(pe, state_rdy, n * 4 + 4)
                for k in range(GS):
                    for c in range(2):
                        h = slice(c * HALF, (c + 1) * HALF)
                        last = pe.matmul(ps_r[h, k * D:(k + 1) * D], state[h, k, :], ident[h, h],
                                         start=True, stop=True)
                last.then_inc(back_mm, 1)

            def turn_x2(r):
                pe.wait_ge(x2p_rdy, r + 1)
                for s in range(GS):
                    last = pe.transpose(ps_rh[:, s * T:(s + 1) * T],
                                        x2_parts[:, s, :, :].rearrange("p a d -> p (a d)"), ident_h[:, :])
                last.then_inc(xsT_mm, 1)

            def gate(r):
                pe.wait_ge(xs_rdy, r + 1)
                for s in range(GS):
                    x = XS[:, bass.ds(r * GT + s * T, T)]
                    pe.matmul(ps_r[:, s * E1:(s + 1) * E1], x, gate_hi[:, :], start=True, stop=False)
                    last = pe.matmul(ps_r[:, s * E1:(s + 1) * E1], x, gate_lo[:, :], start=False, stop=True)
                last.then_inc(logit_mm, 1)

            def up(m, e):
                if after_first(m) or e > 1:
                    pe.wait_ge(gelu_rdy, m * 8 + (e - 1))
                if e == 0:
                    pe.wait_ge(xs_rdy, m + 1)
                xs = XS[:, bass.ts(m, GT)]
                pe.matmul(ps_up[e % 2][:, :], w1_hi[:, e * H1:(e + 1) * H1], xs, start=True, stop=False)
                pe.matmul(ps_up[e % 2][:, :], w1_lo[:, e * H1:(e + 1) * H1], xs, start=False,
                          stop=True).then_inc(up_mm, 1)

            def down(m, e):
                p = e // 2
                if e % 2 == 0:
                    if after_first(m) or p > 1:
                        pe.wait_ge(prod_rdy, m * 4 + (p - 1))
                    pe.matmul(ps_dn[p % 2][:, :], ones3[:, :],
                              b2_parts[:, 2 * p * D:(2 * p + 2) * D].unsqueeze(1).broadcast_to([96, GS, 2 * D]),
                              start=True, stop=False, skip_group_check=True)
                pe.wait_ge(gelu_rdy, m * 8 + (e + 1))
                for s in range(GS):
                    c = s * 2 * D + (e % 2) * D
                    last = pe.matmul(ps_dn[p % 2][:, c:c + D], hT[:, e % 4, s * T:(s + 1) * T],
                                     w("w2")[:, e * D:(e + 1) * D], start=False, stop=True, skip_group_check=True)
                last.then_inc(dn_mm, 1)

            def front(i):
                step(embed, i)
                step(down, i - 4, 2)
                step(rnn_step, i - 2, 2)
                step(turn_x2, i - 3)
                step(up, i - 4, 5)
                step(down, i - 4, 3)
                step(rnn_step, i - 2, 3)
                step(up, i - 4, 6)
                step(gate, i - 3)
                step(down, i - 4, 4)
                step(up, i - 4, 7)
                step(states_back, i - 2)
                step(down, i - 4, 5)
                step(up, i - 3, 0)
                step(down, i - 4, 6)
                step(project, i)
                step(turn_x1, i - 1)
                step(up, i - 3, 1)
                step(gather, i)
                step(up, i - 3, 2)
                step(rnn_input, i - 1)
                step(down, i - 4, 7)
                step(down, i - 3, 0)
                step(up, i - 3, 3)
                step(down, i - 3, 1)
                step(rnn_step, i - 1, 1)
                step(up, i - 3, 4)

            run(pe, front, 4)

            def turn_x3(a):
                wait_pos(pe, ctx_rdy, a)
                hold(pe, x3_rdy, a + 1)
                for s in range(GS):
                    last = pe.transpose(ps_t[0:D, s * T:(s + 1) * T], x3[:, s, 0:D], ident[:, :])
                last.then_inc(x3T_mm, 1)

            def scores(a):
                pe.wait_ge(x3T_rdy, a + 1)
                for s in range(GS):
                    xt = x3T[:, s * T:(s + 1) * T]
                    last = pe.matmul(ps_t[:, s * T:(s + 1) * T], xt, xt, start=True, stop=True)
                last.then_inc(s_mm, 1)

            def context(a):
                pe.wait_ge(exp_rdy, a + 1)
                for s in range(GS):
                    last = pe.matmul(ps_t[:, s * (D + 1):(s + 1) * (D + 1)], expS[:, s, :], x3[:, s, :],
                                     start=True, stop=True)
                last.then_inc(ctx_mm, 1)

            def turn_x4(f):
                wait_pos(pe, rlog_rdy, f)
                hold(pe, x4p_rdy, f + 1)
                for s in range(GS):
                    last = pe.transpose(ps_rh[:, s * T:(s + 1) * T],
                                        x4_parts[:, s, :, :].rearrange("p a d -> p (a d)"), ident_h[:, :])
                last.then_inc(xs4T_mm, 1)

            def router(f):
                pe.wait_ge(xs4_rdy, f + 1)
                for s in range(GS):
                    x = XS[:, bass.ds(f * GT + s * T, T)]
                    pe.matmul(ps_r[:, s * E2:(s + 1) * E2], x, rout_hi[:, :], start=True, stop=False)
                    last = pe.matmul(ps_r[:, s * E2:(s + 1) * E2], x, rout_lo[:, :], start=False, stop=True)
                last.then_inc(rlog_mm, 1)

            def turn_route(f):
                wait_pos(pe, routeT_rdy, f)
                hold(pe, route_rdy, f + 1)
                for s in range(GS):
                    last = pe.transpose(ps_xb[0:3 * E2, s * T:(s + 1) * T],
                                        route[:, s, :, :].rearrange("p a e -> p (a e)"), ident_b[:, :])
                last.then_inc(routeT_mm, 1)

            def first(f, c):
                if c == 0:
                    pe.wait_ge(routeT_rdy, f + 1)
                if after_first(f):
                    pe.wait_ge(f1_act, f * 4 + (c - 3))
                cols, dst = slice(c * P, (c + 1) * P), ps_f1[c][:, :]
                xs, rt = XS[:, bass.ts(f, GT)], RT[:, bass.ts(f, GT)]
                pe.matmul(dst, f1_pick[:, cols], rt, start=True, stop=False)
                pe.matmul(dst, f1_hi[:, cols], xs, start=False, stop=False)
                pe.matmul(dst, f1_lo[:, cols], xs, start=False, stop=True).then_inc(f1_mm, 1)

            def second(f, c):
                if c == 0:
                    wait_pos(pe, fin_rdy, f)
                    for s in range(GS):
                        pe.matmul(ps_x[:, s * D:(s + 1) * D], RT[:, bass.ds(f * GT + s * T, T)], f2_bias[:, :],
                                  start=(s == 0), stop=False, skip_group_check=True)
                pe.wait_ge(f1_act, f * 4 + (c + 1))
                for s in range(GS):
                    last = pe.matmul(ps_x[:, s * D:(s + 1) * D], f1[:, c, s * T:(s + 1) * T],
                                     w("f2")[:, c * D:(c + 1) * D], start=False, stop=(c == CH - 1),
                                     skip_group_check=True)
                if c == CH - 1:
                    last.then_inc(f2_mm, 1)

            def back(i):
                step(first, i - 4, 0)
                step(scores, i - 1)
                step(router, i - 3)
                step(second, i - 5, 3)
                step(first, i - 4, 1)
                step(context, i - 1)
                step(first, i - 4, 2)
                step(second, i - 4, 0)
                step(first, i - 4, 3)
                step(turn_route, i - 3)
                step(turn_x3, i)
                step(second, i - 4, 1)
                step(turn_x4, i - 2)
                step(second, i - 4, 2)

            run(pe, back, 5)

        @block.vector
        def _(dve):
            steps = {"pos": 0, "prep": 0}

            def link(ins, s, key):
                steps[key] += 1
                ins.then_inc(s, 1)
                dve.wait_ge(s, steps[key])

            dve.wait_ge(tok_ld, 32)
            dve.wait_ge(consts, 1)
            link(dve.tensor_scalar(mask_r[:, :], tok_i[:, :], 0.0, None, ALU.not_equal), pos_steps, "pos")
            link(dve.reduce_sum(length[:, :], mask_r[:, :], AX.X), pos_steps, "pos")
            link(dve.tensor_scalar(pos_a[:, :], t_row[:, :], -1.0, length[:, :], ALU.mult, ALU.add), pos_steps, "pos")
            link(dve.tensor_scalar(pos_n[:, :], pos_a[:, :], 0.0, float(VROWS), ALU.is_lt, ALU.mult), pos_steps, "pos")
            link(dve.tensor_tensor(pos_w[:, :], pos_a[:, :], pos_n[:, :], ALU.add), pos_steps, "pos")
            link(dve.tensor_scalar(tok_z[:, :], tok_ci[:, :], 0.0, 0.5, ALU.is_equal, ALU.mult), pos_steps, "pos")
            link(dve.tensor_tensor(tok_c[:, :], tok_ci[:, :], tok_z[:, :], ALU.add), pos_steps, "pos")
            link(dve.tensor_tensor(pos_h[:, :], pos_w[:, :], mask_r[:, :], ALU.mult), pos_steps, "pos")
            dve.wait_ge(w_ld, 32)
            dve.wait_ge(ids, 5)
            for h in range(2):
                q = slice(h * HALF, (h + 1) * HALF)
                dve.tensor_copy(whh_bd[q, q], w("w_hh")[q, :])

            def halves(hi, lo, name):
                link(dve.tensor_scalar(w(name), w(name), WS, None, ALU.mult), prep_a, "prep")
                link(dve.tensor_copy(hi[:, :], w(name)), prep_a, "prep")
                link(dve.tensor_tensor(lo[:, :], w(name), hi[:, :], ALU.subtract), prep_a, "prep")

            halves(w1_hi, w1_lo, "w1")
            halves(gate_hi, gate_lo, "gate")
            halves(rout_hi, rout_lo, "rout")
            halves(f1_hi, f1_lo, "f1")
            q = [slice(k * E2, (k + 1) * E2) for k in range(3)]
            link(dve.scalar_tensor_tensor(out=part[:, :], in0=w("f1b")[0:3 * E2, :], scalar=WS, in1=own[:, :],
                                          op0=ALU.mult, op1=ALU.mult), prep_a, "prep")
            link(dve.tensor_scalar(own[0:E2, :], own[0:E2, :], -1.0, BIG, ALU.add, ALU.mult), prep_a, "prep")
            link(dve.tensor_copy(f1_pick[:, :], part[:, :]), prep_a, "prep")
            link(dve.tensor_tensor(part2[:, :], part[:, :], f1_pick[:, :], ALU.subtract), prep_a, "prep")
            link(dve.tensor_copy(f1_pick[q[1], :], part2[q[1], :]), prep_a, "prep")
            link(dve.tensor_copy(f1_pick[q[2], :], part2[q[2], :]), prep_a, "prep")
            link(dve.tensor_tensor(part[q[2], :], part2[q[2], :], f1_pick[q[2], :], ALU.subtract), prep_a, "prep")
            link(dve.tensor_copy(f1_pick[q[2], :], part[q[2], :]), prep_a, "prep")
            link(dve.tensor_tensor(f1_pick[q[0], :], f1_pick[q[0], :], own[q[0], :], ALU.add), prep_a, "prep")
            fb = w("f2b")[0:3 * E2, :]
            link(dve.tensor_copy(f2_bias[:, :], fb), prep_a, "prep")
            link(dve.tensor_tensor(bpart[:, :], fb, f2_bias[:, :], ALU.subtract), prep_a, "prep")
            link(dve.tensor_copy(f2_bias[q[1], :], bpart[q[1], :]), prep_a, "prep")
            link(dve.tensor_copy(f2_bias[q[2], :], bpart[q[2], :]), prep_a, "prep")
            link(dve.tensor_tensor(bpart[q[2], :], bpart[q[2], :], f2_bias[q[2], :], ALU.subtract), prep_a, "prep")
            link(dve.tensor_copy(f2_bias[q[2], :], bpart[q[2], :]), prep_a, "prep")
            link(dve.tensor_copy(emb_p[:, 0, :], w("emb")), prep_a, "prep")
            link(dve.tensor_tensor(emb_r[:, :], w("emb"), emb_p[:, 0, :], ALU.subtract), prep_a, "prep")
            link(dve.tensor_copy(emb_p[:, 1, :], emb_r[:, :]), prep_a, "prep")
            link(dve.tensor_tensor(emb_r[:, :], emb_r[:, :], emb_p[:, 1, :], ALU.subtract), prep_a, "prep")
            link(dve.tensor_copy(emb_p[:, 2, :], emb_r[:, :]), prep_a, "prep")
            for src, left, dst in ((emb_last[:, :], bpart, emb_lp), (w("b2")[0:96, :], b2_rest, b2_parts)):
                link(dve.tensor_copy(dst[:, :], src), prep_a, "prep")
                link(dve.tensor_tensor(left[:, :], src, dst[:, :], ALU.subtract), prep_a, "prep")
                link(dve.tensor_copy(dst[q[1], :], left[q[1], :]), prep_a, "prep")
                link(dve.tensor_copy(dst[q[2], :], left[q[2], :]), prep_a, "prep")
                link(dve.tensor_tensor(left[q[2], :], left[q[2], :], dst[q[2], :], ALU.subtract), prep_a, "prep")
                link(dve.tensor_copy(dst[q[2], :], left[q[2], :]), prep_a, "prep")
            for k in range(3):
                row = slice(k * 32, k * 32 + 1)
                dve.memset(ones3[row, :], 1.0)
                dve.tensor_copy(emb_l[row, :], emb_lp[row, :])
            dve.tensor_tensor(rnn_bias[:, :], w("b_ih"), w("b_hh"), ALU.add).then_inc(prep, 1)

            def stats_in(g, k, after):
                if after_first(g):
                    hold(dve, ln_ve[k], g)
                if after is not None:
                    hold(dve, after, g + 1)
                for s in range(GS):
                    last = dve.bn_stats(bn[k][:, s, :], Hg(g)[:, s * D:(s + 1) * D])
                last.then_inc(ln_bn[k], 1)

            def stats_out(g, k):
                hold(dve, ln_bn[k], g + 1)
                for s in range(GS):
                    last = dve.bn_aggr(mv[k][:, s, :], bn[k][:, s, :])
                last.then_inc(ln_mv[k], 1)

            def high_half(g, x, parts, x_sem, free, done):
                wait_pos(dve, free, g)
                dve.wait_ge(x_sem, g + 1)
                dve.tensor_copy(parts[:, :, 0, :], x[:, :, :]).then_inc(done, 1)

            def low_half(g, x, parts, hi_sem, done):
                dve.wait_ge(hi_sem, g + 1)
                dve.tensor_tensor(parts[:, :, 1, :], x[:, :, :], parts[:, :, 0, :], ALU.subtract).then_inc(done, 1)

            def one_hot(t):
                dve.wait_ge(grp_ld, t * 32 + 32)
                wait_pos(dve, pe_mm, t)
                pos = pos_b[:, bass.ts(t, GT)]
                dve.tensor_scalar(onehot[:, :], pos, part_id[:, :], None, ALU.is_equal)
                dve.tensor_scalar(onehot_l[:, :], pos[0:96, :], float(T), None, ALU.is_equal).then_inc(onehot_rdy, 1)

            def equal_tokens(t, s):
                if s == 0:
                    wait_pos(dve, gath_mm, t)
                ins = dve.scalar_tensor_tensor(
                    out=graph[:, s, :], in0=tok_b[:, bass.ds(t * GT + s * T, T)],
                    scalar=tok_c[:, bass.ds(t * GS + s, 1)], in1=later[:, :], op0=ALU.is_equal, op1=ALU.mult)
                if s == GS - 1:
                    ins.then_inc(graph_rdy, 1)

            def degree(t):
                sums = ps_t[:, 0:GS * (D + 1)].rearrange("p (s d) -> p s d", s=GS)
                dve.wait_ge(gath_mm, t + 1)
                dve.tensor_scalar(deg[:, :], sums[:, :, D], 1.0, None, ALU.max).then_inc(deg_rdy, 1)

            def inverse_degree(t):
                dve.wait_ge(deg_rdy, t + 1)
                dve.reciprocal(rdeg[:, :], deg[:, :]).then_inc(rdeg_rdy, 1)

            def embedded(t):
                dve.wait_ge(rdeg_rdy, t + 1)
                for s in range(GS):
                    last = dve.scalar_tensor_tensor(
                        out=Hg(t)[:, s * D:(s + 1) * D], in0=ps_t[:, s * (D + 1):s * (D + 1) + D],
                        scalar=rdeg[:, s:s + 1], in1=w("b_oah"), op0=ALU.mult, op1=ALU.add)
                last.then_inc(h1_rdy, 1)

            def add_states(r):
                dve.wait_ge(back_mm, r + 1)
                dve.tensor_tensor(Hg(r), ps_r[:, 0:GD], Hg(r), ALU.add).then_inc(h2_rdy, 1)

            def top2(r, k):
                at = r * TOP_STEPS + k
                if k == 0:
                    dve.wait_ge(logit_mm, r + 1)
                    dve.scalar_tensor_tensor(
                        out=logit[:, :, :], in0=ps_r[:, 0:GS * E1].rearrange("p (s e) -> p s e", s=GS),
                        scalar=1.0 / WS, in1=over_s(w("gate_b"), P, E1), op0=ALU.mult, op1=ALU.add).then_inc(logit_rdy, 1)
                elif k == 1:
                    dve.wait_ge(logit_rdy, r + 1)
                    dve.tensor_reduce(lmax[:, 0, :], logit[:, :, :], AX.X, ALU.max).then_inc(top_steps, 1)
                elif k == 2:
                    dve.wait_ge(top_steps, at - 1)
                    dve.tensor_tensor(ldiff[:, :, :], logit[:, :, :], over_e(lmax[:, 0, :], E1),
                                      ALU.subtract).then_inc(ldiff_rdy, 1)
                elif k == 3:
                    dve.wait_ge(ldiff_rdy, r + 1)
                    dve.scalar_tensor_tensor(out=cand[:, :, :], in0=ldiff[:, :, :], scalar=0.0, in1=rank8[:, :, :],
                                             op0=ALU.is_equal, op1=ALU.mult).then_inc(top_steps, 1)
                elif k == 4:
                    dve.wait_ge(top_steps, at - 2)
                    dve.tensor_reduce(lmax[:, 1, :], cand[:, :, :], AX.X, ALU.max).then_inc(top_steps, 1)
                elif k == 5:
                    dve.wait_ge(top_steps, at - 2)
                    dve.tensor_tensor(pick1[:, :, :], cand[:, :, :], over_e(lmax[:, 1, :], E1),
                                      ALU.is_equal).then_inc(top_steps, 1)
                elif k == 6:
                    dve.wait_ge(top_steps, at - 2)
                    dve.scalar_tensor_tensor(out=rest[:, :, :], in0=pick1[:, :, :], scalar=-BIG,
                                             in1=ldiff[:, :, :], op0=ALU.mult, op1=ALU.add).then_inc(top_steps, 1)
                elif k == 7:
                    dve.wait_ge(top_steps, at - 2)
                    dve.tensor_reduce(lmax[:, 2, :], rest[:, :, :], AX.X, ALU.max).then_inc(top_steps, 1)
                elif k == 8:
                    dve.wait_ge(top_steps, at - 2)
                    dve.tensor_tensor(cand2[:, :, :], rest[:, :, :], over_e(lmax[:, 2, :], E1),
                                      ALU.is_equal).then_inc(top_steps, 1)
                elif k == 9:
                    dve.wait_ge(top_steps, at - 2)
                    dve.tensor_tensor(rank2[:, :, :], cand2[:, :, :], rank8[:, :, :], ALU.mult).then_inc(top_steps, 1)
                elif k == 10:
                    dve.wait_ge(top_steps, at - 2)
                    dve.tensor_reduce(lmax[:, 3, :], rank2[:, :, :], AX.X, ALU.max).then_inc(top_steps, 1)
                elif k == 11:
                    dve.wait_ge(top_steps, at - 2)
                    dve.tensor_tensor(pick2[:, :, :], rank2[:, :, :], over_e(lmax[:, 3, :], E1),
                                      ALU.is_equal).then_inc(top_steps, 1)
                elif k == 12:
                    dve.wait_ge(top_steps, at - 2)
                    dve.tensor_tensor(picks[:, :, :], pick1[:, :, :], pick2[:, :, :], ALU.add).then_inc(top_steps, 1)

            def softmax8(r, k):
                at = r * SM_STEPS + k
                if k == 0:
                    dve.wait_ge(lth_rdy, r + 1)
                    dve.tensor_scalar(lden[:, :, :], lth[:, :, :], -1.0, 1.0, ALU.mult, ALU.add).then_inc(sm_steps, 1)
                elif k == 1:
                    dve.wait_ge(sm_steps, at)
                    dve.reciprocal(lrec[:, :, :], lden[:, :, :]).then_inc(sm_steps, 1)
                elif k == 2:
                    dve.wait_ge(sm_steps, at)
                    dve.scalar_tensor_tensor(out=lroot[:, 0, :, :], in0=lth[:, :, :], scalar=1.0, in1=lrec[:, :, :],
                                             op0=ALU.add, op1=ALU.mult).then_inc(sm_steps, 1)
                elif k == 3:
                    dve.wait_ge(sm_steps, at)
                    dve.tensor_tensor(lroot[:, 1, :, :], lroot[:, 0, :, :], lroot[:, 0, :, :],
                                      ALU.mult).then_inc(sm_steps, 1)
                elif k == 4:
                    dve.wait_ge(sm_steps, at)
                    dve.tensor_tensor(lexp[:, :, :], lroot[:, 1, :, :], lroot[:, 1, :, :],
                                      ALU.mult).then_inc(sm_steps, 1)
                elif k == 5:
                    dve.wait_ge(sm_steps, at)
                    dve.tensor_reduce(lmax[:, 4, :], lexp[:, :, :], AX.X, ALU.add).then_inc(sm_steps, 1)
                elif k == 6:
                    dve.wait_ge(sm_steps, at)
                    dve.reciprocal(lmax[:, 5, :], lmax[:, 4, :]).then_inc(sm_steps, 1)
                elif k == 7:
                    dve.wait_ge(top_steps, (r + 1) * TOP_STEPS)
                    dve.tensor_tensor(lpick[:, :, :], lexp[:, :, :], picks[:, :, :], ALU.mult).then_inc(sm_steps, 1)
                elif k == 8:
                    dve.wait_ge(sm_steps, at)
                    dve.tensor_tensor(CW[:, bass.ts(r, GS * E1)].rearrange("p (s e) -> p s e", s=GS),
                                      lpick[:, :, :], over_e(lmax[:, 5, :], E1), ALU.mult).then_inc(sm_steps, 1)

            def weigh(m, p):
                if p == 0:
                    hold(dve, sm_steps, (m + 1) * SM_STEPS)
                dve.wait_ge(dn_mm, m * 8 + (2 * p + 2))
                if after_first(m) or p > 1:
                    dve.wait_ge(sum_b, m * 4 + (p - 1))
                cw = CW[:, bass.ts(m, GS * E1)].rearrange("p (s e) -> p s e", s=GS)[:, :, 2 * p:2 * p + 2]
                dve.tensor_tensor(prod[:, p % 2, :, :, :],
                                  ps_dn[p % 2][:, :].rearrange("p (s k d) -> p s k d", s=GS, k=2),
                                  cw.unsqueeze(3).broadcast_to([P, GS, 2, D]), ALU.mult).then_inc(prod_rdy, 1)

            def front(i):
                step(top2, i - 5, 11)
                step(softmax8, i - 5, 5)
                step(top2, i - 5, 12)
                step(softmax8, i - 5, 6)
                step(equal_tokens, i - 1, 2)
                step(softmax8, i - 5, 7)
                step(softmax8, i - 5, 8)
                step(weigh, i - 5, 0)
                step(one_hot, i)
                step(top2, i - 4, 0)
                step(top2, i - 4, 1)
                step(equal_tokens, i - 1, 3)
                step(weigh, i - 5, 1)
                step(top2, i - 4, 2)
                step(top2, i - 4, 3)
                step(top2, i - 4, 4)
                step(add_states, i - 3)
                step(stats_in, i - 3, "moe", h2_rdy)
                step(stats_out, i - 3, "moe")
                step(top2, i - 4, 5)
                step(top2, i - 4, 6)
                step(top2, i - 4, 7)
                step(softmax8, i - 4, 0)
                step(top2, i - 4, 8)
                step(softmax8, i - 4, 1)
                step(weigh, i - 5, 2)
                step(degree, i - 1)
                step(top2, i - 4, 9)
                step(inverse_degree, i - 1)
                step(softmax8, i - 4, 2)
                step(embedded, i - 1)
                step(stats_in, i - 1, "rnn", h1_rdy)
                step(softmax8, i - 4, 3)
                step(stats_out, i - 1, "rnn")
                step(equal_tokens, i, 0)
                step(weigh, i - 5, 3)
                step(top2, i - 4, 10)
                step(high_half, i - 3, x2, x2_parts, x2_rdy, xsT_mm, hi2_rdy)
                step(low_half, i - 3, x2, x2_parts, hi2_rdy, x2p_rdy)
                step(equal_tokens, i, 1)
                step(softmax8, i - 4, 4)

            run(dve, front, 5)

            def router_logits(f):
                dve.wait_ge(rlog_mm, f + 1)
                dve.scalar_tensor_tensor(out=rlog[:, :, :], in0=ps_r[:, 0:GS * E2].rearrange("p (s e) -> p s e", s=GS),
                                         scalar=1.0 / WS, in1=over_s(w("rout_b"), P, E2), op0=ALU.mult,
                                         op1=ALU.add).then_inc(rlog_rdy, 1)

            def top1(f, k):
                at = f * RT_STEPS + k
                if k == 0:
                    dve.wait_ge(rlog_rdy, f + 1)
                    dve.tensor_reduce(rmax[:, 0, :], rlog[:, :, :], AX.X, ALU.max).then_inc(rt_steps, 1)
                elif k == 1:
                    dve.wait_ge(rt_steps, at)
                    dve.tensor_tensor(req[:, :, :], rlog[:, :, :], over_e(rmax[:, 0, :], E2),
                                      ALU.is_equal).then_inc(rt_steps, 1)
                elif k == 2:
                    dve.wait_ge(rt_steps, at)
                    dve.tensor_tensor(rrank[:, :, :], req[:, :, :], rank32[:, :, :], ALU.mult).then_inc(rt_steps, 1)
                elif k == 3:
                    dve.wait_ge(rt_steps, at)
                    dve.tensor_reduce(rmax[:, 1, :], rrank[:, :, :], AX.X, ALU.max).then_inc(rt_steps, 1)
                elif k == 4:
                    dve.wait_ge(rt_steps, at)
                    wait_pos(dve, routeT_mm, f)
                    for c in range(3):
                        last = dve.tensor_tensor(route[:, :, c, :], rrank[:, :, :], over_e(rmax[:, 1, :], E2),
                                                 ALU.is_equal)
                    last.then_inc(route_rdy, 1)

            def weight_sum(a):
                dve.wait_ge(ctx_mm, a + 1)
                dve.reciprocal(rden[:, :], ps_t[:, 0:GS * (D + 1)].rearrange("p (s d) -> p s d", s=GS)[:, :, D]
                               ).then_inc(den_rdy, 1)

            def context_out(a):
                dve.wait_ge(den_rdy, a + 1)
                wait_pos(dve, h4_rdy, a)
                dve.tensor_tensor(ctxn[:, :, :], ps_t[:, 0:GS * (D + 1)].rearrange("p (s d) -> p s d", s=GS)[:, :, 0:D],
                                  over_d(rden[:, :]), ALU.mult).then_inc(ctx_rdy, 1)

            def finish(f):
                dve.wait_ge(f2_mm, f + 1)
                dve.scalar_tensor_tensor(out=Hg3(f), in0=ps_x[:, 0:GD].rearrange("p (s d) -> p s d", s=GS),
                                         scalar=0.0, in1=Hg3(f), op0=ALU.max, op1=ALU.add).then_inc(fin_rdy, 1)

            def back(i):
                step(stats_out, i - 1, "att")
                step(top1, i - 5, 3)
                step(weight_sum, i - 3)
                step(top1, i - 5, 4)
                step(context_out, i - 3)
                step(high_half, i - 4, x4, x4_parts, x4_rdy, xs4T_mm, hi4_rdy)
                step(low_half, i - 4, x4, x4_parts, hi4_rdy, x4p_rdy)
                step(stats_in, i - 3, "ffn", h4_rdy)
                step(stats_out, i - 3, "ffn")
                step(stats_in, i, "att", None)
                step(router_logits, i - 4)
                step(top1, i - 4, 0)
                step(finish, i - 6)
                step(top1, i - 4, 1)
                step(top1, i - 4, 2)

            dve.wait_ge(sum_b, 4 * NG)
            run(dve, back, 6)


def kernel(**inputs):
    import numpy as _np
    import concourse.bacc as _bacc
    from concourse import mybir as _mybir
    from concourse.bass_utils import run_bass_kernel_spmd as _run

    x = {k: _np.ascontiguousarray(v) for k, v in inputs.items()}
    P = 128
    up, down = x["L0_ffn_W1"], x["L0_ffn_W2"]
    f_up, f_down = x["L1_ffn_W1"], x["L1_ffn_W2"]

    def twice(a):
        return _np.concatenate([a, a], 0)

    def every(a):
        return _np.tile(a.reshape(1, -1), (P, 1))

    def four(a):
        return _np.tile(a, (4, 1))

    pieces = {
        "emb": x["L0_tok_emb_table"][:P],
        "w_in": twice(x["L0_tok_W_in"].T),
        "w_ih": twice(x["L0_attn_W_ih"].T),
        "w_hh": twice(x["L0_attn_W_hh"].T),
        "b_ih": twice(x["L0_attn_b_ih"].reshape(-1, 1)),
        "b_hh": twice(x["L0_attn_b_hh"].reshape(-1, 1)),
        "b_oah": every(x["L0_tok_b_oah"]),
        "w1": twice(up.transpose(1, 0, 2).reshape(64, -1)),
        "b1": x["L0_ffn_b1"].T,
        "w2": down.transpose(1, 0, 2).reshape(P, -1),
        "b2": every(x["L0_ffn_b2"]),
        "gate": twice(x["L0_ffn_gate_w"]),
        "gate_b": every(x["L0_ffn_gate_b"]),
        "rout": twice(x["L1_ffn_router_w"].T),
        "rout_b": every(x["L1_ffn_router_b"]),
        "f1": twice(f_up.transpose(1, 0, 2).reshape(64, -1)),
        "f1b": every(x["L1_ffn_b1"]),
        "f2": f_down.reshape(4, P, 64).transpose(1, 0, 2).reshape(P, -1),
        "f2b": four(x["L1_ffn_b2"]),
    }
    cols, at = {}, 0
    for name, piece in pieces.items():
        cols[name] = (at, piece.shape[1])
        at += piece.shape[1]
    cols["_total"] = at
    weights = _np.ascontiguousarray(_np.concatenate(list(pieces.values()), 1))
    arrays = {
        "tok": x["x"],
        "tok_cols": _np.ascontiguousarray(x["x"].T),
        "weights": weights,
        "emb_tail": _np.tile(x["L0_tok_emb_table"][P:], (96, 1)),
    }
    nc = _bacc.Bacc("TRN2", target_bir_lowering=False, num_devices=1)
    args = [nc.dram_tensor(n, a.shape, _mybir.dt.from_np(a.dtype), kind="ExternalInput").ap() for n, a in arrays.items()]
    out = nc.dram_tensor("out", (64, 128, 64), _mybir.dt.float32, kind="ExternalOutput").ap()
    lm_tower_kernel(nc, *args, out, cols)
    r = _run(nc, [arrays], core_ids=[0])
    return r.results[0]["out"]
```

```python
import concourse.bass as bass
from concourse import mybir
from contextlib import ExitStack


def lm_tower_kernel(nc, tok, tok_cols, weights, emb_tail, out, COLS):
    fp32, bf16, fp16, i32 = (mybir.dt.float32, mybir.dt.bfloat16, mybir.dt.float16, mybir.dt.int32)
    ALU = mybir.AluOpType
    ACT = mybir.ActivationFunctionType
    AX = mybir.AxisListType

    P = 128
    B, T = tok.shape
    D = 64
    HALF = P // 2
    VROWS = T + 1
    GS = 4
    NG = B // GS
    GT = GS * T
    GD = GS * D
    E1, H1 = 8, 128
    E2, H2 = 32, 16
    CH = E2 * H2 // P
    WS = 256.0
    BIG = 2.0 ** 100
    EPS_LN = 1e-5
    EPS_NORM_SQ = 1e-24

    ctx = ExitStack()
    with ctx:
        def sb(name, shape, dt):
            return ctx.enter_context(nc.sbuf_tensor(name, shape, dt))

        def bank(name):
            return ctx.enter_context(nc.psum_tensor(name, [P, 512], fp32))

        def sem(name):
            return ctx.enter_context(nc.semaphore(name))

        W = sb("W", [P, COLS["_total"]], fp32)

        def w(name):
            a, n = COLS[name]
            return W[:, a:a + n]

        emb_last = sb("emb_last", [3 * 32, D], fp32)
        emb_p = sb("emb_p", [P, 2, D], fp16)
        emb_lp = sb("emb_lp", [3 * 32, D], fp16)
        emb_l = sb("emb_l", [3 * 32, D], fp16)
        b2_parts = sb("b2_parts", [3 * 32, E1 * D], bf16)
        b2_rest = sb("b2_rest", [3 * 32, E1 * D], fp32)
        ones3 = sb("ones3", [3 * 32, P], bf16)
        whh_bd = sb("whh_bd", [P, P], fp32)
        rnn_bias = sb("rnn_bias", [P, 1], fp32)
        w1_hi = sb("w1_hi", [P, E1 * H1], fp16)
        w1_lo = sb("w1_lo", [P, E1 * H1], fp16)
        w2_hi = sb("w2_hi", [P, E1 * D], fp16)
        w2_lo = sb("w2_lo", [P, E1 * D], fp16)
        gate_hi = sb("gate_hi", [P, E1], fp16)
        gate_lo = sb("gate_lo", [P, E1], fp16)
        rout_hi = sb("rout_hi", [P, E2], fp16)
        rout_lo = sb("rout_lo", [P, E2], fp16)
        f1_hi = sb("f1_hi", [P, CH * P], fp16)
        f1_lo = sb("f1_lo", [P, CH * P], fp16)
        f2_hi = sb("f2_hi", [P, CH * D], fp16)
        f2_lo = sb("f2_lo", [P, CH * D], fp16)
        f1_pick = sb("f1_pick", [3 * E2, CH * P], bf16)
        f2_bias = sb("f2_bias", [3 * E2, D], bf16)
        own = sb("own", [3 * E2, CH * P], fp32)
        part = sb("part", [3 * E2, CH * P], fp32)
        part2 = sb("part2", [3 * E2, CH * P], fp32)
        bpart = sb("bpart", [3 * E2, D], fp32)
        ident = sb("ident", [P, P], fp32)
        ident_h = sb("ident_h", [P, P], fp16)
        ident_b = sb("ident_b", [P, P], bf16)
        later = sb("later", [P, T], fp32)
        part_id = sb("part_id", [P, 1], fp32)
        t_row = sb("t_row", [B, T], fp32)
        rank8 = sb("rank8", [P, GS, E1], fp32)
        rank32 = sb("rank32", [P, GS, E2], fp32)
        neg_half = sb("neg_half", [P, GS], fp32)
        warm = sb("warm", [P, GS], fp32)
        tok_i = sb("tok_i", [B, T], i32)
        tok_ci = sb("tok_ci", [P, B], i32)
        tok_c = sb("tok_c", [P, B], fp32)
        tok_z = sb("tok_z", [P, B], fp32)
        mask_r = sb("mask_r", [B, T], fp32)
        length = sb("length", [B, 1], fp32)
        pos_a = sb("pos_a", [B, T], fp32)
        pos_n = sb("pos_n", [B, T], fp32)
        pos_w = sb("pos_w", [B, T], fp32)
        pos_h = sb("pos_h", [B, T], bf16)
        tok_b = sb("tok_b", [P, B * T], i32)
        pos_b = sb("pos_b", [P, B * T], bf16)
        pos_dram = nc.dram_tensor("pos_scratch", [B, T], bf16, kind="Internal").ap()
        H = sb("H", [P, NG * GD], fp32)
        XS = sb("XS", [P, NG * GT], fp16)
        CW = sb("CW", [P, NG * GS * E1], fp32)
        onehot = sb("onehot", [P, GT], fp16)
        onehot_l = sb("onehot_l", [3 * 32, GT], fp16)
        graph = sb("graph", [P, GS, T], fp16)
        peT = sb("peT", [D, GT], fp32)
        pe_sq = sb("pe_sq", [D, GT], fp32)
        pe_ss = sb("pe_ss", [D, GS], fp32)
        pe_sc = sb("pe_sc", [D, GS], fp32)
        pe_rn = sb("pe_rn", [D, GS], fp32)
        w_in_n = sb("w_in_n", [D, GS, D], fp32)
        hn_hi = sb("hn_hi", [P, GS, D + 1], fp16)
        hn_lo = sb("hn_lo", [P, GS, D], fp16)
        deg = sb("deg", [P, GS], fp32)
        rdeg = sb("rdeg", [P, GS], fp32)
        x1 = sb("x1", [P, GS, D], fp32)
        x1T = sb("x1T", [D, GT], fp32)
        state = sb("state", [P, GS, HALF], fp32)
        x2 = sb("x2", [P, GS, D], fp32)
        x2_parts = sb("x2_parts", [P, GS, 2, D], fp16)
        logit = sb("logit", [P, GS, E1], fp32)
        ldiff = sb("ldiff", [P, GS, E1], fp32)
        lexp = sb("lexp", [P, GS, E1], fp32)
        cand = sb("cand", [P, GS, E1], fp32)
        pick1 = sb("pick1", [P, GS, E1], fp32)
        rest = sb("rest", [P, GS, E1], fp32)
        cand2 = sb("cand2", [P, GS, E1], fp32)
        pick2 = sb("pick2", [P, GS, E1], fp32)
        rank2 = sb("rank2", [P, GS, E1], fp32)
        picks = sb("picks", [P, GS, E1], fp32)
        lrec = sb("lrec", [P, GS, E1], fp32)
        lpick = sb("lpick", [P, GS, E1], fp32)
        lmax = sb("lmax", [P, 6, GS], fp32)
        lth = sb("lth", [P, GS, E1], fp32)
        lden = sb("lden", [P, GS, E1], fp32)
        lroot = sb("lroot", [P, 2, GS, E1], fp32)
        hT = sb("hT", [P, 4, GT], fp32)
        hTh = sb("hTh", [P, 2, GT], fp16)
        hTl = sb("hTl", [P, 2, GT], fp16)
        prod = sb("prod", [P, 2, GS, 2, D], fp32)
        LN = ("rnn", "moe", "att", "ffn")
        bn = {k: sb(f"bn_{k}", [P, GS, 6], fp32) for k in LN}
        mv = {k: sb(f"mv_{k}", [P, GS, 2], fp32) for k in LN}
        ve = {k: sb(f"ve_{k}", [P, GS], fp32) for k in LN}
        nm = {k: sb(f"nm_{k}", [P, GS], fp32) for k in LN}
        nmr = {k: sb(f"nmr_{k}", [P, GS], fp32) for k in LN}
        rstd = {k: sb(f"rstd_{k}", [P, GS], fp32) for k in LN}
        x3 = sb("x3", [P, GS, D + 1], fp32)
        x3T = sb("x3T", [D, GT], fp32)
        expS = sb("expS", [P, GS, T], fp32)
        rden = sb("rden", [P, GS], fp32)
        ctxn = sb("ctxn", [P, GS, D], fp32)
        x4_s = sb("x4_s", [P, GS, D], fp32)
        x4 = sb("x4", [P, GS, D], fp32)
        x4_parts = sb("x4_parts", [P, GS, 2, D], fp16)
        rlog = sb("rlog", [P, GS, E2], fp32)
        req = sb("req", [P, GS, E2], fp32)
        rrank = sb("rrank", [P, GS, E2], fp32)
        rmax = sb("rmax", [P, 2, GS], fp32)
        route = sb("route", [P, GS, 3, E2], bf16)
        RT = sb("RT", [3 * E2, NG * GT], bf16)
        f1h = sb("f1h", [P, CH, GT], fp16)
        f1l = sb("f1l", [P, CH, GT], fp16)
        y = sb("y", [P, GD], fp32)

        ps_xp = bank("ps_xp")
        ps_t = bank("ps_t")
        ps_r = bank("ps_r")
        ps_up = [bank(f"ps_up{i}") for i in range(2)]
        ps_dn = [bank(f"ps_dn{i}") for i in range(2)]
        ps_x = bank("ps_x")
        ps_f1 = [ps_up[0], ps_up[1], ps_dn[0], ps_dn[1]]
        ps_rh = ps_r[:, 0:256].bitcast(fp16)
        ps_xb = ps_xp[:, 0:256].bitcast(bf16)

        w_ld, w_late, tok_ld, pos_st, grp_ld, out_st = (sem(n) for n in ("w_ld", "w_late", "tok_ld", "pos_st", "grp_ld", "out_st"))
        consts, ids, prep, prep_a, prep_b, prep_up, prep_down, prep_back, pos_steps = (sem(n) for n in (
            "consts", "ids", "prep", "prep_a", "prep_b", "prep_up", "prep_down", "prep_back", "pos_steps"))
        onehot_rdy, graph_rdy, pe_mm, peT_rdy, ss_rdy, pool_t, win_rdy = (sem(n) for n in (
            "onehot_rdy", "graph_rdy", "pe_mm", "peT_rdy", "ss_rdy", "pool_t", "win_rdy"))
        hn_mm, hn_hi_rdy, hn_rdy, gath_mm, deg_rdy, rdeg_rdy, h1_rdy = (sem(n) for n in (
            "hn_mm", "hn_hi_rdy", "hn_rdy", "gath_mm", "deg_rdy", "rdeg_rdy", "h1_rdy"))
        x1_rdy, x1T_mm, x1T_rdy, xp_mm, step_mm, state_rdy, back_mm = (sem(n) for n in (
            "x1_rdy", "x1T_mm", "x1T_rdy", "xp_mm", "step_mm", "state_rdy", "back_mm"))
        ln_bn = {k: sem(f"ln_bn_{k}") for k in LN}
        ln_mv = {k: sem(f"ln_mv_{k}") for k in LN}
        ln_ve = {k: sem(f"ln_ve_{k}") for k in LN}
        ln_pw = {k: sem(f"ln_pw_{k}") for k in LN}
        ln_rs = {k: sem(f"ln_rs_{k}") for k in LN}
        h2_rdy, x2_rdy, hi2_rdy, x2p_rdy, xsT_mm, xs_rdy, logit_mm, logit_rdy = (sem(n) for n in (
            "h2_rdy", "x2_rdy", "hi2_rdy", "x2p_rdy", "xsT_mm", "xs_rdy", "logit_mm", "logit_rdy"))
        ldiff_rdy, lth_rdy, top_steps, sm_steps = (sem(n) for n in ("ldiff_rdy", "lth_rdy", "top_steps", "sm_steps"))
        up_mm, gelu_rdy, high_rdy, low_rdy, dn_mm, prod_rdy, sum_a, sum_b = (sem(n) for n in (
            "up_mm", "gelu_rdy", "high_rdy", "low_rdy", "dn_mm", "prod_rdy", "sum_a", "sum_b"))
        x3_rdy, x3T_mm, x3T_rdy, s_mm, exp_rdy, ctx_mm, den_rdy, ctx_rdy, h4_rdy = (sem(n) for n in (
            "x3_rdy", "x3T_mm", "x3T_rdy", "s_mm", "exp_rdy", "ctx_mm", "den_rdy", "ctx_rdy", "h4_rdy"))
        x4_scaled, x4_rdy, hi4_rdy, x4p_rdy, xs4T_mm, xs4_rdy, rlog_mm, rlog_rdy, rt_steps, route_rdy = (sem(n) for n in (
            "x4_scaled", "x4_rdy", "hi4_rdy", "x4p_rdy", "xs4T_mm", "xs4_rdy", "rlog_mm", "rlog_rdy", "rt_steps", "route_rdy"))
        routeT_mm, routeT_rdy, f1_mm, relu_rdy, rest_rdy, f2_mm, y_rdy, fin_rdy = (sem(n) for n in (
            "routeT_mm", "routeT_rdy", "f1_mm", "relu_rdy", "rest_rdy", "f2_mm", "y_rdy", "fin_rdy"))

        TOP_STEPS, SM_STEPS, RT_STEPS = 11, 9, 4

        def Hg(g):
            return H[:, bass.ts(g, GD)]

        def Hg3(g):
            return Hg(g).rearrange("p (s d) -> p s d", s=GS)

        def over_d(ap):
            return ap.unsqueeze(2).broadcast_to([ap.shape[0], GS, D])

        def over_e(ap, e):
            return ap.unsqueeze(2).broadcast_to([P, GS, e])

        def over_s(ap, rows, n):
            return ap.unsqueeze(1).broadcast_to([rows, GS, n])

        def wait_pos(eng, s, v):
            if not isinstance(v, int) or v > 0:
                eng.wait_ge(s, v)

        def hold(eng, s, v):
            eng.wait_ge(s, v)
            if not isinstance(v, int):
                eng.nop(nofuse=True)

        def run(eng, round_, top, between=()):
            for i in range(top + 1):
                round_(i)
                if i < len(between) and between[i]:
                    between[i]()
            with eng.Fori(top + 1, NG) as i:
                round_(i)
            for i in range(NG, NG + top):
                round_(i)

        def step(work, g, *args):
            if not isinstance(g, int) or 0 <= g < NG:
                work(g, *args)

        def after_first(g):
            return not isinstance(g, int) or g > 0

        block = ctx.enter_context(nc.Block())

        @block.sync
        def _(sp):
            sp.dma_start(tok_i[:, :], tok).then_inc(tok_ld, 16)
            sp.dma_start(tok_ci[:, :], tok_cols).then_inc(tok_ld, 16)
            early = COLS["_early"]
            sp.dma_start(W[:, 0:early], weights[:, 0:early]).then_inc(w_ld, 16)
            sp.dma_start(emb_last[:, :], emb_tail).then_inc(w_ld, 16)
            sp.wait_ge(pos_steps, 8)
            sp.dma_start(pos_dram, pos_h[:, :]).then_inc(pos_st, 16)
            sp.wait_ge(pos_st, 16)
            tok_flat = tok.rearrange("b t -> (b t)")
            pos_flat = pos_dram.rearrange("b t -> (b t)")

            def load_group(g):
                sp.dma_start(tok_b[:, bass.ts(g, GT)], tok_flat[bass.ts(g, GT)].partition_broadcast(P)).then_inc(grp_ld, 16)
                sp.dma_start(pos_b[:, bass.ts(g, GT)], pos_flat[bass.ts(g, GT)].partition_broadcast(P)).then_inc(grp_ld, 16)

            load_group(0)
            sp.dma_start(W[:, early:], weights[:, early:]).then_inc(w_late, 16)
            with sp.Fori(1, NG) as g:
                sp.wait_ge(grp_ld, g * 32)
                load_group(g)
            out_v = out.rearrange("b t d -> t b d")
            with sp.Fori(0, NG) as g:
                sp.wait_ge(fin_rdy, g + 1)
                sp.dma_start(out_v[:, bass.ts(g, GS), :], Hg3(g)).then_inc(out_st, 16)
            sp.wait_ge(out_st, 16 * NG)

        @block.gpsimd
        def _(pool):
            steps = {"prep": 0}
            pool.memset(ident[:, :], 0.0)
            pool.memset(own[:, :], 0.0)
            pool.memset(later[:, :], 1.0)
            pool.memset(ones3[:, :], 0.0)
            pool.memset(emb_l[:, :], 0.0)
            pool.memset(neg_half[:, :], -0.5)
            pool.memset(whh_bd[:, :], 0.0)
            pool.memset(state[:, :, :], 0.0)
            pool.memset(hn_hi[:, :, :], WS)
            pool.memset(x3[:, :, :], 1.0)
            pool.iota(t_row[:, :], [[1, T]], base=0, channel_multiplier=0, allow_small_or_imprecise_dtypes=True)
            pool.iota(part_id[:, :], [[0, 1]], base=0, channel_multiplier=1, allow_small_or_imprecise_dtypes=True)
            pool.iota(rank8[:, :, :], [[0, GS], [-1, E1]], base=E1, channel_multiplier=0, allow_small_or_imprecise_dtypes=True)
            pool.iota(rank32[:, :, :], [[0, GS], [-1, E2]], base=E2, channel_multiplier=0,
                      allow_small_or_imprecise_dtypes=True).then_inc(consts, 1)
            pool.wait_ge(consts, 1)
            pool.affine_select(out=ident[:, :], in_=ident[:, :], compare_op=ALU.not_equal, fill=1.0, base=0,
                               pattern=[[-1, P]], channel_multiplier=1)
            pool.affine_select(out=later[:, :], in_=later[:, :], compare_op=ALU.is_ge, fill=0.0, base=0,
                               pattern=[[-1, T]], channel_multiplier=1).then_inc(ids, 1)
            for k in range(3):
                pool.wait_ge(ids, k + 1)
                o = own[k * E2:(k + 1) * E2, :].rearrange("p (e h) -> p e h", h=H2)
                pool.affine_select(out=o, in_=o, compare_op=ALU.not_equal, fill=1.0, base=0,
                                   pattern=[[-1, E2], [0, H2]], channel_multiplier=1).then_inc(ids, 1)
            pool.wait_ge(ids, 4)
            pool.tensor_copy(ident_h[:, :], ident[:, :])
            pool.tensor_copy(ident_b[:, :], ident[:, :]).then_inc(ids, 1)

            def link(ins):
                steps["prep"] += 1
                ins.then_inc(prep_b, 1)
                pool.wait_ge(prep_b, steps["prep"])

            def halves(hi, lo, name):
                link(pool.tensor_scalar(w(name), w(name), WS, None, ALU.mult))
                link(pool.tensor_copy(hi[:, :], w(name)))
                link(pool.tensor_tensor(lo[:, :], w(name), hi[:, :], ALU.subtract))

            def prepare_router():
                pool.wait_ge(w_late, 16)
                halves(rout_hi, rout_lo, "rout")
                halves(f2_hi, f2_lo, "f2")

            def prepare_first():
                halves(f1_hi, f1_lo, "f1")

            def rstd_of(g, k, used):
                wait_pos(pool, ln_rs[k], g)
                hold(pool, ln_mv[k], g + 1)
                pool.tensor_scalar(ve[k][:, :], mv[k][:, :, 1], EPS_LN, None, ALU.add)
                pool.tensor_scalar(nm[k][:, :], mv[k][:, :, 0], -1.0, None, ALU.mult).then_inc(ln_ve[k], 1)
                wait_pos(pool, used, g)
                pool.wait_ge(ln_ve[k], g + 1)
                pool.tensor_tensor(rstd[k][:, :], ve[k][:, :], neg_half[:, :], ALU.pow).then_inc(ln_pw[k], 1)
                pool.wait_ge(ln_pw[k], g + 1)
                pool.tensor_tensor(nmr[k][:, :], nm[k][:, :], rstd[k][:, :], ALU.mult).then_inc(ln_rs[k], 1)

            def expert_sum(m, p):
                k = p % 2
                if after_first(m) or p > 0:
                    pool.wait_ge(sum_b, m * 4 + p)
                hold(pool, prod_rdy, m * 4 + (p + 1))
                pool.tensor_tensor(Hg3(m), Hg3(m), prod[:, k, :, 0, :], ALU.add).then_inc(sum_a, 1)
                hold(pool, sum_a, m * 4 + (p + 1))
                pool.tensor_tensor(Hg3(m), Hg3(m), prod[:, k, :, 1, :], ALU.add).then_inc(sum_b, 1)

            def scale_w_in(t):
                hold(pool, ss_rdy, t + 1)
                pool.tensor_scalar(pe_sc[:, :], pe_ss[:, :], EPS_NORM_SQ, None, ALU.max).then_inc(pool_t, 1)
                pool.wait_ge(pool_t, t * 2 + 1)
                pool.tensor_tensor(pe_rn[:, :], pe_sc[:, :], neg_half[0:D, :], ALU.pow).then_inc(pool_t, 1)
                pool.wait_ge(pool_t, t * 2 + 2)
                wait_pos(pool, hn_mm, t)
                pool.tensor_tensor(w_in_n[:, :, :], over_s(w("w_in")[0:D, :], D, D), over_d(pe_rn[:, :]),
                                   ALU.mult).then_inc(win_rdy, 1)

            def front(i):
                step(rstd_of, i - 1, "rnn", x1_rdy)
                step(scale_w_in, i)
                step(expert_sum, i - 4, 1)
                step(rstd_of, i - 2, "moe", x2_rdy)
                step(expert_sum, i - 4, 2)
                step(expert_sum, i - 4, 3)
                step(expert_sum, i - 3, 0)

            run(pool, front, 4, (prepare_router, prepare_first))

            def add_context(a):
                hold(pool, ctx_rdy, a + 1)
                pool.tensor_tensor(Hg3(a), Hg3(a), ctxn[:, :, :], ALU.add).then_inc(h4_rdy, 1)

            def normalise_ffn(f):
                wait_pos(pool, x4p_rdy, f)
                hold(pool, ln_rs["ffn"], f + 1)
                pool.tensor_tensor(x4_s[:, :, :], Hg3(f), over_d(rstd["ffn"][:, :]), ALU.mult).then_inc(x4_scaled, 1)
                hold(pool, x4_scaled, f + 1)
                pool.tensor_tensor(x4[:, :, :], x4_s[:, :, :], over_d(nmr["ffn"][:, :]), ALU.add).then_inc(x4_rdy, 1)

            def finish(f):
                hold(pool, y_rdy, f + 1)
                pool.tensor_tensor(Hg(f), Hg(f), y[:, :], ALU.add).then_inc(fin_rdy, 1)

            def back(i):
                step(rstd_of, i - 3, "ffn", x4_rdy)
                step(normalise_ffn, i - 3)
                step(add_context, i - 2)
                step(finish, i - 7)
                step(rstd_of, i, "att", x3_rdy)

            run(pool, back, 7)

        @block.scalar
        def _(act):
            def normalise(g, k, dst, free, done):
                wait_pos(act, free, g)
                act.wait_ge(ln_rs[k], g + 1)
                for s in range(GS):
                    last = act.activation(dst[:, s, 0:D], Hg(g)[:, s * D:(s + 1) * D], ACT.Identity,
                                          bias=nmr[k][:, s:s + 1], scale=rstd[k][:, s:s + 1])
                last.then_inc(done, 1)

            def pe_squares(t):
                act.wait_ge(pe_mm, t + 1)
                wait_pos(act, win_rdy, t)
                for s in range(GS):
                    last = act.activation(pe_sq[:, s * T:(s + 1) * T], ps_t[0:D, s * T:(s + 1) * T], ACT.Square,
                                          scale=1.0 / WS, accum_out=pe_ss[:, s:s + 1])
                last.then_inc(ss_rdy, 1)

            def pe_out(t):
                act.wait_ge(pe_mm, t + 1)
                wait_pos(act, hn_mm, t)
                act.activation(peT[:, :], ps_t[0:D, :], ACT.Copy, scale=1.0 / WS).then_inc(peT_rdy, 1)

            def hn_out(t):
                act.wait_ge(hn_mm, t + 1)
                wait_pos(act, gath_mm, t)
                act.activation(hn_hi[:, :, 0:D], ps_t[:, 0:GD].rearrange("p (s d) -> p s d", s=GS),
                               ACT.Copy, scale=WS).then_inc(hn_hi_rdy, 1)

            def x1T_out(n):
                act.wait_ge(x1T_mm, n + 1)
                wait_pos(act, xp_mm, n)
                act.activation(x1T[:, :], ps_x[0:D, :], ACT.Copy).then_inc(x1T_rdy, 1)

            def tanh(n, k):
                act.wait_ge(step_mm, n * 4 + (k + 1))
                if k == 0:
                    wait_pos(act, back_mm, n)
                act.activation(state[:, k, :], ps_xp[:, k * HALF:(k + 1) * HALF], ACT.Tanh,
                               bias=rnn_bias[:, :]).then_inc(state_rdy, 1)

            def xs_out(r):
                act.wait_ge(xsT_mm, r + 1)
                act.activation(XS[:, bass.ts(r, GT)], ps_rh, ACT.Copy).then_inc(xs_rdy, 1)

            def logit_tanh(r):
                act.wait_ge(ldiff_rdy, r + 1)
                act.activation(lth[:, :, :], ldiff[:, :, :], ACT.Tanh, scale=1.0 / 8).then_inc(lth_rdy, 1)

            def gelu(m, e):
                act.wait_ge(up_mm, m * 8 + (e + 1))
                if after_first(m) or e > 3:
                    act.wait_ge(dn_mm, m * 8 + (e - 3))
                act.activation(hT[:, e % 4, :], ps_up[e % 2][:, :], ACT.Gelu, bias=w("b1")[:, e:e + 1],
                               scale=1.0 / WS).then_inc(gelu_rdy, 1)

            def hidden_high(m, e):
                act.wait_ge(gelu_rdy, m * 8 + (e + 1))
                act.activation(hTh[:, e // 2 % 2, :], hT[:, e % 4, :], ACT.Copy).then_inc(high_rdy, 1)

            def front(i):
                step(normalise, i - 2, "rnn", x1, x1T_mm, x1_rdy)
                step(pe_out, i - 1)
                step(gelu, i - 4, 1)
                step(logit_tanh, i - 4)
                step(hidden_high, i - 4, 1)
                step(gelu, i - 4, 2)
                step(x1T_out, i - 2)
                step(hn_out, i - 1)
                step(gelu, i - 4, 3)
                step(hidden_high, i - 4, 3)
                step(normalise, i - 3, "moe", x2, x2p_rdy, x2_rdy)
                step(tanh, i - 2, 0)
                step(gelu, i - 4, 4)
                step(gelu, i - 4, 5)
                step(hidden_high, i - 4, 5)
                step(tanh, i - 2, 1)
                step(gelu, i - 4, 6)
                step(xs_out, i - 3)
                step(tanh, i - 2, 2)
                step(gelu, i - 4, 7)
                step(hidden_high, i - 4, 7)
                step(tanh, i - 2, 3)
                step(pe_squares, i)
                step(gelu, i - 3, 0)

            act.wait_ge(consts, 1)
            act.activation(warm[:, :], neg_half[:, :], ACT.Gelu)
            act.wait_ge(prep, 1)
            run(act, front, 4)

            def x3T_out(a):
                act.wait_ge(x3T_mm, a + 1)
                wait_pos(act, s_mm, a)
                act.activation(x3T[:, :], ps_t[0:D, :], ACT.Copy).then_inc(x3T_rdy, 1)

            def exp(a):
                act.wait_ge(s_mm, a + 1)
                wait_pos(act, ctx_mm, a)
                act.activation(expS[:, :, :].rearrange("p s t -> p (s t)"), ps_t[:, :], ACT.Exp,
                               scale=float(D) ** -0.5).then_inc(exp_rdy, 1)

            def xs4_out(f):
                act.wait_ge(xs4T_mm, f + 1)
                act.activation(XS[:, bass.ts(f, GT)], ps_rh, ACT.Copy).then_inc(xs4_rdy, 1)

            def route_out(f):
                act.wait_ge(routeT_mm, f + 1)
                act.activation(RT[:, bass.ts(f, GT)], ps_xb[0:3 * E2, :], ACT.Copy).then_inc(routeT_rdy, 1)

            def high_half(f):
                wait_pos(act, xs4T_mm, f)
                act.wait_ge(x4_rdy, f + 1)
                act.activation(x4_parts[:, :, 0, :], x4[:, :, :], ACT.Copy).then_inc(hi4_rdy, 1)

            def relu(f, c):
                act.wait_ge(f1_mm, f * 4 + (c + 1))
                if after_first(f):
                    act.wait_ge(f2_mm, f * 4 + (c - 3))
                act.activation(f1h[:, c, :], ps_f1[c][:, :], ACT.Relu).then_inc(relu_rdy, 1)

            def back(i):
                step(xs4_out, i - 3)
                step(exp, i - 1)
                step(relu, i - 5, 2)
                step(route_out, i - 4)
                step(relu, i - 5, 3)
                step(normalise, i, "att", x3, ctx_mm, x3_rdy)
                step(high_half, i - 2)
                step(relu, i - 4, 0)
                step(x3T_out, i)
                step(relu, i - 4, 1)

            run(act, back, 5)

        @block.tensor
        def _(pe):
            pe.wait_ge(ids, 5)
            pe.wait_ge(w_ld, 32)
            pe.wait_ge(prep, 1)

            def embed(t):
                wait_pos(pe, h1_rdy, t)
                pe.wait_ge(onehot_rdy, t + 1)
                for k in range(2):
                    pe.matmul(ps_t[0:D, :], emb_p[:, k, :], onehot[:, :], start=(k == 0), stop=False)
                pe.matmul(ps_t[0:D, :], emb_l[:, :], onehot_l[:, :], start=False, stop=True).then_inc(pe_mm, 1)

            def project(t):
                pe.wait_ge(win_rdy, t + 1)
                pe.wait_ge(peT_rdy, t + 1)
                for s in range(GS):
                    last = pe.matmul(ps_t[:, s * D:(s + 1) * D], peT[:, s * T:(s + 1) * T], w_in_n[:, s, :],
                                     start=True, stop=True)
                last.then_inc(hn_mm, 1)

            def gather(t):
                pe.wait_ge(graph_rdy, t + 1)
                pe.wait_ge(hn_rdy, t + 1)
                for s in range(GS):
                    a = s * (D + 1)
                    pe.matmul(ps_t[:, a:a + D + 1], graph[:, s, :], hn_hi[:, s, :], start=True, stop=False)
                    last = pe.matmul(ps_t[:, a:a + D], graph[:, s, :], hn_lo[:, s, :], start=False, stop=True)
                last.then_inc(gath_mm, 1)

            def turn_x1(n):
                wait_pos(pe, x1T_rdy, n)
                hold(pe, x1_rdy, n + 1)
                for s in range(GS):
                    last = pe.transpose(ps_x[0:D, s * T:(s + 1) * T], x1[:, s, :], ident[:, :])
                last.then_inc(x1T_mm, 1)

            def rnn_step(n, k):
                if k:
                    pe.wait_ge(state_rdy, n * 4 + k)
                prev = (k - 1) % GS
                pe.matmul(ps_xp[:, k * HALF:(k + 1) * HALF], whh_bd[:, :], state[:, prev, :], start=False,
                          stop=True, skip_group_check=True).then_inc(step_mm, 1)

            def rnn_input(n):
                pe.wait_ge(x1T_rdy, n + 1)
                if after_first(n):
                    hold(pe, state_rdy, n * 4)
                xin = x1T[:, :].rearrange("p (s c t) -> p c s t", s=GS, c=2)
                for c in range(2):
                    last = pe.matmul(ps_xp[c * HALF:(c + 1) * HALF, 0:GS * HALF], w("w_ih")[0:D, :], xin[:, c],
                                     start=True, stop=False, skip_group_check=True)
                last.then_inc(xp_mm, 1)
                rnn_step(n, 0)

            def states_back(n):
                wait_pos(pe, logit_rdy, n)
                hold(pe, state_rdy, n * 4 + 4)
                for k in range(GS):
                    for c in range(2):
                        h = slice(c * HALF, (c + 1) * HALF)
                        last = pe.matmul(ps_r[h, k * D:(k + 1) * D], state[h, k, :], ident[h, h],
                                         start=True, stop=True)
                last.then_inc(back_mm, 1)

            def turn_x2(r):
                pe.wait_ge(x2p_rdy, r + 1)
                for s in range(GS):
                    last = pe.transpose(ps_rh[:, s * T:(s + 1) * T],
                                        x2_parts[:, s, :, :].rearrange("p a d -> p (a d)"), ident_h[:, :])
                last.then_inc(xsT_mm, 1)

            def gate(r):
                if isinstance(r, int) and r == 0:
                    pe.wait_ge(prep_up, 1)
                pe.wait_ge(xs_rdy, r + 1)
                for s in range(GS):
                    x = XS[:, bass.ds(r * GT + s * T, T)]
                    pe.matmul(ps_r[:, s * E1:(s + 1) * E1], x, gate_hi[:, :], start=True, stop=False)
                    last = pe.matmul(ps_r[:, s * E1:(s + 1) * E1], x, gate_lo[:, :], start=False, stop=True)
                last.then_inc(logit_mm, 1)

            def up(m, e):
                if after_first(m) or e > 1:
                    pe.wait_ge(gelu_rdy, m * 8 + (e - 1))
                if e == 0:
                    if isinstance(m, int) and m == 0:
                        pe.wait_ge(prep_up, 1)
                    pe.wait_ge(xs_rdy, m + 1)
                xs = XS[:, bass.ts(m, GT)]
                pe.matmul(ps_up[e % 2][:, :], w1_hi[:, e * H1:(e + 1) * H1], xs, start=True, stop=False)
                pe.matmul(ps_up[e % 2][:, :], w1_lo[:, e * H1:(e + 1) * H1], xs, start=False,
                          stop=True).then_inc(up_mm, 1)

            def down(m, e):
                p = e // 2
                if isinstance(m, int) and m == 0 and e == 0:
                    pe.wait_ge(prep_down, 1)
                if e % 2 == 0:
                    if after_first(m) or p > 1:
                        pe.wait_ge(prod_rdy, m * 4 + (p - 1))
                    pe.matmul(ps_dn[p % 2][:, :], ones3[:, :],
                              b2_parts[:, 2 * p * D:(2 * p + 2) * D].unsqueeze(1).broadcast_to([96, GS, 2 * D]),
                              start=True, stop=False, skip_group_check=True)
                cols = slice(e * D, (e + 1) * D)
                if e % 2 == 0:
                    pe.wait_ge(gelu_rdy, m * 8 + (e + 1))
                    terms = ((hT[:, e % 4, :], w("w2")[:, cols]),)
                else:
                    pe.wait_ge(low_rdy, m * 4 + (p + 1))
                    high, low = hTh[:, p % 2, :], hTl[:, p % 2, :]
                    terms = ((high, w2_hi[:, cols]), (high, w2_lo[:, cols]), (low, w2_hi[:, cols]))
                for s in range(GS):
                    c = s * 2 * D + (e % 2) * D
                    for hid, wgt in terms:
                        last = pe.matmul(ps_dn[p % 2][:, c:c + D], hid[:, s * T:(s + 1) * T], wgt, start=False,
                                         stop=True, skip_group_check=True)
                last.then_inc(dn_mm, 1)

            def front(i):
                step(turn_x1, i - 2)
                step(project, i - 1)
                step(up, i - 4, 3)
                step(down, i - 4, 0)
                step(up, i - 4, 4)
                step(down, i - 4, 1)
                step(rnn_input, i - 2)
                step(gather, i - 1)
                step(up, i - 4, 5)
                step(down, i - 4, 2)
                step(rnn_step, i - 2, 1)
                step(up, i - 4, 6)
                step(down, i - 4, 3)
                step(turn_x2, i - 3)
                step(up, i - 4, 7)
                step(rnn_step, i - 2, 2)
                step(embed, i)
                step(down, i - 4, 4)
                step(rnn_step, i - 2, 3)
                step(gate, i - 3)
                step(up, i - 3, 0)
                step(down, i - 4, 5)
                step(states_back, i - 2)
                step(up, i - 3, 1)
                step(down, i - 4, 6)
                step(up, i - 3, 2)
                step(down, i - 4, 7)

            run(pe, front, 4)

            def turn_x3(a):
                wait_pos(pe, ctx_rdy, a)
                hold(pe, x3_rdy, a + 1)
                for s in range(GS):
                    last = pe.transpose(ps_t[0:D, s * T:(s + 1) * T], x3[:, s, 0:D], ident[:, :])
                last.then_inc(x3T_mm, 1)

            def scores(a):
                pe.wait_ge(x3T_rdy, a + 1)
                for s in range(GS):
                    xt = x3T[:, s * T:(s + 1) * T]
                    last = pe.matmul(ps_t[:, s * T:(s + 1) * T], xt, xt, start=True, stop=True)
                last.then_inc(s_mm, 1)

            def context(a):
                pe.wait_ge(exp_rdy, a + 1)
                for s in range(GS):
                    last = pe.matmul(ps_t[:, s * (D + 1):(s + 1) * (D + 1)], expS[:, s, :], x3[:, s, :],
                                     start=True, stop=True)
                last.then_inc(ctx_mm, 1)

            def turn_x4(f):
                wait_pos(pe, rlog_rdy, f)
                hold(pe, x4p_rdy, f + 1)
                for s in range(GS):
                    last = pe.transpose(ps_rh[:, s * T:(s + 1) * T],
                                        x4_parts[:, s, :, :].rearrange("p a d -> p (a d)"), ident_h[:, :])
                last.then_inc(xs4T_mm, 1)

            def router(f):
                if isinstance(f, int) and f == 0:
                    pe.wait_ge(prep_b, 9)
                pe.wait_ge(xs4_rdy, f + 1)
                for s in range(GS):
                    x = XS[:, bass.ds(f * GT + s * T, T)]
                    pe.matmul(ps_r[:, s * E2:(s + 1) * E2], x, rout_hi[:, :], start=True, stop=False)
                    last = pe.matmul(ps_r[:, s * E2:(s + 1) * E2], x, rout_lo[:, :], start=False, stop=True)
                last.then_inc(rlog_mm, 1)

            def turn_route(f):
                wait_pos(pe, routeT_rdy, f)
                hold(pe, route_rdy, f + 1)
                for s in range(GS):
                    last = pe.transpose(ps_xb[0:3 * E2, s * T:(s + 1) * T],
                                        route[:, s, :, :].rearrange("p a e -> p (a e)"), ident_b[:, :])
                last.then_inc(routeT_mm, 1)

            def first(f, c):
                if c == 0:
                    if isinstance(f, int) and f == 0:
                        pe.wait_ge(prep_back, 1)
                    pe.wait_ge(routeT_rdy, f + 1)
                if after_first(f):
                    pe.wait_ge(rest_rdy, f * 4 + (c - 3))
                cols, dst = slice(c * P, (c + 1) * P), ps_f1[c][:, :]
                xs, rt = XS[:, bass.ts(f, GT)], RT[:, bass.ts(f, GT)]
                pe.matmul(dst, f1_pick[:, cols], rt, start=True, stop=False)
                pe.matmul(dst, f1_hi[:, cols], xs, start=False, stop=False)
                pe.matmul(dst, f1_lo[:, cols], xs, start=False, stop=True).then_inc(f1_mm, 1)

            def second(f, c):
                if c == 0:
                    wait_pos(pe, y_rdy, f)
                    for s in range(GS):
                        pe.matmul(ps_x[:, s * D:(s + 1) * D], RT[:, bass.ds(f * GT + s * T, T)], f2_bias[:, :],
                                  start=(s == 0), stop=False, skip_group_check=True)
                pe.wait_ge(rest_rdy, f * 4 + (c + 1))
                for s in range(GS):
                    for hid, wgt in ((f1h, f2_hi), (f1h, f2_lo), (f1l, f2_hi)):
                        last = pe.matmul(ps_x[:, s * D:(s + 1) * D], hid[:, c, s * T:(s + 1) * T],
                                         wgt[:, c * D:(c + 1) * D], start=False, stop=(c == CH - 1),
                                         skip_group_check=True)
                last.then_inc(f2_mm, 1)

            def back(i):
                step(router, i - 3)
                step(context, i - 1)
                step(second, i - 5, 0)
                step(second, i - 5, 1)
                step(first, i - 4, 0)
                step(second, i - 5, 2)
                step(first, i - 4, 1)
                step(turn_x3, i)
                step(second, i - 5, 3)
                step(first, i - 4, 2)
                step(turn_x4, i - 2)
                step(scores, i)
                step(first, i - 4, 3)
                step(turn_route, i - 3)

            run(pe, back, 5)

        @block.vector
        def _(dve):
            steps = {"pos": 0, "prep": 0}

            def link(ins, s, key):
                steps[key] += 1
                ins.then_inc(s, 1)
                dve.wait_ge(s, steps[key])

            dve.wait_ge(tok_ld, 32)
            dve.wait_ge(consts, 1)
            link(dve.tensor_scalar(mask_r[:, :], tok_i[:, :], 0.0, None, ALU.not_equal), pos_steps, "pos")
            link(dve.reduce_sum(length[:, :], mask_r[:, :], AX.X), pos_steps, "pos")
            link(dve.tensor_scalar(pos_a[:, :], t_row[:, :], -1.0, length[:, :], ALU.mult, ALU.add), pos_steps, "pos")
            link(dve.tensor_scalar(pos_n[:, :], pos_a[:, :], 0.0, float(VROWS), ALU.is_lt, ALU.mult), pos_steps, "pos")
            link(dve.tensor_tensor(pos_w[:, :], pos_a[:, :], pos_n[:, :], ALU.add), pos_steps, "pos")
            link(dve.tensor_scalar(tok_z[:, :], tok_ci[:, :], 0.0, 0.5, ALU.is_equal, ALU.mult), pos_steps, "pos")
            link(dve.tensor_tensor(tok_c[:, :], tok_ci[:, :], tok_z[:, :], ALU.add), pos_steps, "pos")
            link(dve.tensor_tensor(pos_h[:, :], pos_w[:, :], mask_r[:, :], ALU.mult), pos_steps, "pos")
            dve.wait_ge(w_ld, 32)
            dve.wait_ge(ids, 1)
            for h in range(2):
                q = slice(h * HALF, (h + 1) * HALF)
                dve.tensor_copy(whh_bd[q, q], w("w_hh")[q, :])
            link(dve.tensor_scalar(w("emb"), w("emb"), WS, None, ALU.mult), prep_a, "prep")
            link(dve.tensor_copy(emb_p[:, 0, :], w("emb")), prep_a, "prep")
            link(dve.tensor_tensor(emb_p[:, 1, :], w("emb"), emb_p[:, 0, :], ALU.subtract), prep_a, "prep")
            link(dve.tensor_scalar(emb_last[:, :], emb_last[:, :], WS, None, ALU.mult), prep_a, "prep")
            link(dve.tensor_copy(emb_lp[:, :], emb_last[:, :]), prep_a, "prep")
            dve.tensor_copy(emb_l[0:1, :], emb_lp[0:1, :])
            dve.tensor_tensor(emb_l[32:33, :], emb_last[32:33, :], emb_lp[32:33, :], ALU.subtract)
            dve.tensor_tensor(rnn_bias[:, :], w("b_ih"), w("b_hh"), ALU.add).then_inc(prep, 1)

            def halves(hi, lo, name):
                link(dve.tensor_scalar(w(name), w(name), WS, None, ALU.mult), prep_a, "prep")
                link(dve.tensor_copy(hi[:, :], w(name)), prep_a, "prep")
                return dve.tensor_tensor(lo[:, :], w(name), hi[:, :], ALU.subtract)

            def prepare_up():
                dve.wait_ge(w_late, 16)
                link(halves(gate_hi, gate_lo, "gate"), prep_a, "prep")
                halves(w1_hi, w1_lo, "w1").then_inc(prep_up, 1)

            def prepare_down():
                link(halves(w2_hi, w2_lo, "w2"), prep_a, "prep")
                q = [slice(k * 32, (k + 1) * 32) for k in range(3)]
                b2 = w("b2")[0:96, :]
                link(dve.tensor_scalar(b2, b2, WS, None, ALU.mult), prep_a, "prep")
                link(dve.tensor_copy(b2_parts[:, :], b2), prep_a, "prep")
                link(dve.tensor_tensor(b2_rest[:, :], b2, b2_parts[:, :], ALU.subtract), prep_a, "prep")
                link(dve.tensor_copy(b2_parts[q[1], :], b2_rest[q[1], :]), prep_a, "prep")
                link(dve.tensor_copy(b2_parts[q[2], :], b2_rest[q[2], :]), prep_a, "prep")
                link(dve.tensor_tensor(b2_rest[q[2], :], b2_rest[q[2], :], b2_parts[q[2], :], ALU.subtract), prep_a, "prep")
                link(dve.tensor_copy(b2_parts[q[2], :], b2_rest[q[2], :]), prep_a, "prep")
                for k in range(3):
                    last = dve.memset(ones3[k * 32:k * 32 + 1, :], 1.0)
                last.then_inc(prep_down, 1)

            def prepare_first_bias():
                dve.wait_ge(ids, 5)
                q = [slice(k * E2, (k + 1) * E2) for k in range(3)]
                b1 = w("f1b")[0:3 * E2, :]
                link(dve.tensor_scalar(b1, b1, WS, None, ALU.mult), prep_a, "prep")
                link(dve.tensor_tensor(part[:, :], b1, own[:, :], ALU.mult), prep_a, "prep")
                link(dve.tensor_scalar(own[q[0], :], own[q[0], :], -1.0, BIG, ALU.add, ALU.mult), prep_a, "prep")
                link(dve.tensor_copy(f1_pick[:, :], part[:, :]), prep_a, "prep")
                link(dve.tensor_tensor(part2[:, :], part[:, :], f1_pick[:, :], ALU.subtract), prep_a, "prep")
                link(dve.tensor_copy(f1_pick[q[1], :], part2[q[1], :]), prep_a, "prep")
                link(dve.tensor_copy(f1_pick[q[2], :], part2[q[2], :]), prep_a, "prep")
                link(dve.tensor_tensor(part[q[2], :], part2[q[2], :], f1_pick[q[2], :], ALU.subtract), prep_a, "prep")
                link(dve.tensor_copy(f1_pick[q[2], :], part[q[2], :]), prep_a, "prep")
                link(dve.tensor_tensor(f1_pick[q[0], :], f1_pick[q[0], :], own[q[0], :], ALU.add), prep_a, "prep")

            def prepare_second_bias():
                q = [slice(k * E2, (k + 1) * E2) for k in range(3)]
                fb = w("f2b")[0:3 * E2, :]
                link(dve.tensor_scalar(fb, fb, WS * WS, None, ALU.mult), prep_a, "prep")
                link(dve.tensor_copy(f2_bias[:, :], fb), prep_a, "prep")
                link(dve.tensor_tensor(bpart[:, :], fb, f2_bias[:, :], ALU.subtract), prep_a, "prep")
                link(dve.tensor_copy(f2_bias[q[1], :], bpart[q[1], :]), prep_a, "prep")
                link(dve.tensor_copy(f2_bias[q[2], :], bpart[q[2], :]), prep_a, "prep")
                link(dve.tensor_tensor(bpart[q[2], :], bpart[q[2], :], f2_bias[q[2], :], ALU.subtract), prep_a, "prep")
                dve.tensor_copy(f2_bias[q[2], :], bpart[q[2], :]).then_inc(prep_back, 1)

            def stats_in(g, k, after, count=1):
                if after_first(g):
                    hold(dve, ln_ve[k], g)
                hold(dve, after, (g + 1) * count)
                for s in range(GS):
                    last = dve.bn_stats(bn[k][:, s, :], Hg(g)[:, s * D:(s + 1) * D])
                last.then_inc(ln_bn[k], 1)

            def stats_out(g, k):
                hold(dve, ln_bn[k], g + 1)
                for s in range(GS):
                    last = dve.bn_aggr(mv[k][:, s, :], bn[k][:, s, :])
                last.then_inc(ln_mv[k], 1)

            def high_half(g, x, parts, x_sem, free, done):
                wait_pos(dve, free, g)
                dve.wait_ge(x_sem, g + 1)
                dve.tensor_copy(parts[:, :, 0, :], x[:, :, :]).then_inc(done, 1)

            def low_half(g, x, parts, hi_sem, done):
                dve.wait_ge(hi_sem, g + 1)
                dve.tensor_tensor(parts[:, :, 1, :], x[:, :, :], parts[:, :, 0, :], ALU.subtract).then_inc(done, 1)

            def one_hot(t):
                dve.wait_ge(grp_ld, t * 32 + 32)
                wait_pos(dve, pe_mm, t)
                pos = pos_b[:, bass.ts(t, GT)]
                dve.tensor_scalar(onehot[:, :], pos, part_id[:, :], None, ALU.is_equal)
                dve.tensor_scalar(onehot_l[:, :], pos[0:96, :], float(T), None, ALU.is_equal).then_inc(onehot_rdy, 1)

            def equal_tokens(t, s):
                if s == 0:
                    wait_pos(dve, gath_mm, t)
                ins = dve.scalar_tensor_tensor(
                    out=graph[:, s, :], in0=tok_b[:, bass.ds(t * GT + s * T, T)],
                    scalar=tok_c[:, bass.ds(t * GS + s, 1)], in1=later[:, :], op0=ALU.is_equal, op1=ALU.mult)
                if s == GS - 1:
                    ins.then_inc(graph_rdy, 1)

            def hn_low(t):
                dve.wait_ge(hn_hi_rdy, t + 1)
                dve.scalar_tensor_tensor(out=hn_lo[:, :, :], in0=ps_t[:, 0:GD].rearrange("p (s d) -> p s d", s=GS),
                                         scalar=WS, in1=hn_hi[:, :, 0:D], op0=ALU.mult,
                                         op1=ALU.subtract).then_inc(hn_rdy, 1)

            def degree(t):
                sums = ps_t[:, 0:GS * (D + 1)].rearrange("p (s d) -> p s d", s=GS)
                dve.wait_ge(gath_mm, t + 1)
                dve.tensor_scalar(deg[:, :], sums[:, :, D], WS, None, ALU.max).then_inc(deg_rdy, 1)

            def inverse_degree(t):
                dve.wait_ge(deg_rdy, t + 1)
                dve.reciprocal(rdeg[:, :], deg[:, :]).then_inc(rdeg_rdy, 1)

            def embedded(t):
                dve.wait_ge(rdeg_rdy, t + 1)
                for s in range(GS):
                    last = dve.scalar_tensor_tensor(
                        out=Hg(t)[:, s * D:(s + 1) * D], in0=ps_t[:, s * (D + 1):s * (D + 1) + D],
                        scalar=rdeg[:, s:s + 1], in1=w("b_oah"), op0=ALU.mult, op1=ALU.add)
                last.then_inc(h1_rdy, 1)

            def add_states(r):
                dve.wait_ge(back_mm, r + 1)
                dve.tensor_tensor(Hg(r), ps_r[:, 0:GD], Hg(r), ALU.add).then_inc(h2_rdy, 1)

            def top2(r, k):
                at = r * TOP_STEPS + k
                if k == 0:
                    dve.wait_ge(logit_mm, r + 1)
                    dve.scalar_tensor_tensor(
                        out=logit[:, :, :], in0=ps_r[:, 0:GS * E1].rearrange("p (s e) -> p s e", s=GS),
                        scalar=1.0 / WS, in1=over_s(w("gate_b"), P, E1), op0=ALU.mult, op1=ALU.add).then_inc(logit_rdy, 1)
                elif k == 1:
                    dve.wait_ge(logit_rdy, r + 1)
                    dve.tensor_reduce(lmax[:, 0, :], logit[:, :, :], AX.X, ALU.max).then_inc(top_steps, 1)
                elif k == 2:
                    dve.wait_ge(top_steps, at - 1)
                    dve.tensor_tensor(ldiff[:, :, :], logit[:, :, :], over_e(lmax[:, 0, :], E1),
                                      ALU.subtract).then_inc(ldiff_rdy, 1)
                elif k == 3:
                    dve.wait_ge(ldiff_rdy, r + 1)
                    dve.scalar_tensor_tensor(out=cand[:, :, :], in0=ldiff[:, :, :], scalar=0.0, in1=rank8[:, :, :],
                                             op0=ALU.is_equal, op1=ALU.mult).then_inc(top_steps, 1)
                elif k == 4:
                    dve.wait_ge(top_steps, at - 2)
                    dve.tensor_reduce(lmax[:, 1, :], cand[:, :, :], AX.X, ALU.max).then_inc(top_steps, 1)
                elif k == 5:
                    dve.wait_ge(top_steps, at - 2)
                    dve.tensor_tensor(pick1[:, :, :], cand[:, :, :], over_e(lmax[:, 1, :], E1),
                                      ALU.is_equal).then_inc(top_steps, 1)
                elif k == 6:
                    dve.wait_ge(top_steps, at - 2)
                    dve.scalar_tensor_tensor(out=rest[:, :, :], in0=pick1[:, :, :], scalar=-BIG,
                                             in1=ldiff[:, :, :], op0=ALU.mult, op1=ALU.add).then_inc(top_steps, 1)
                elif k == 7:
                    dve.wait_ge(top_steps, at - 2)
                    dve.tensor_reduce(lmax[:, 2, :], rest[:, :, :], AX.X, ALU.max).then_inc(top_steps, 1)
                elif k == 8:
                    dve.wait_ge(top_steps, at - 2)
                    dve.tensor_tensor(cand2[:, :, :], rest[:, :, :], over_e(lmax[:, 2, :], E1),
                                      ALU.is_equal).then_inc(top_steps, 1)
                elif k == 9:
                    dve.wait_ge(top_steps, at - 2)
                    dve.tensor_tensor(rank2[:, :, :], cand2[:, :, :], rank8[:, :, :], ALU.mult).then_inc(top_steps, 1)
                elif k == 10:
                    dve.wait_ge(top_steps, at - 2)
                    dve.tensor_reduce(lmax[:, 3, :], rank2[:, :, :], AX.X, ALU.max).then_inc(top_steps, 1)
                elif k == 11:
                    dve.wait_ge(top_steps, at - 2)
                    dve.tensor_tensor(pick2[:, :, :], rank2[:, :, :], over_e(lmax[:, 3, :], E1),
                                      ALU.is_equal).then_inc(top_steps, 1)
                elif k == 12:
                    dve.wait_ge(top_steps, at - 2)
                    dve.tensor_tensor(picks[:, :, :], pick1[:, :, :], pick2[:, :, :], ALU.add).then_inc(top_steps, 1)

            def softmax8(r, k):
                at = r * SM_STEPS + k
                if k == 0:
                    dve.wait_ge(lth_rdy, r + 1)
                    dve.tensor_scalar(lden[:, :, :], lth[:, :, :], -1.0, 1.0, ALU.mult, ALU.add).then_inc(sm_steps, 1)
                elif k == 1:
                    dve.wait_ge(sm_steps, at)
                    dve.reciprocal(lrec[:, :, :], lden[:, :, :]).then_inc(sm_steps, 1)
                elif k == 2:
                    dve.wait_ge(sm_steps, at)
                    dve.scalar_tensor_tensor(out=lroot[:, 0, :, :], in0=lth[:, :, :], scalar=1.0, in1=lrec[:, :, :],
                                             op0=ALU.add, op1=ALU.mult).then_inc(sm_steps, 1)
                elif k == 3:
                    dve.wait_ge(sm_steps, at)
                    dve.tensor_tensor(lroot[:, 1, :, :], lroot[:, 0, :, :], lroot[:, 0, :, :],
                                      ALU.mult).then_inc(sm_steps, 1)
                elif k == 4:
                    dve.wait_ge(sm_steps, at)
                    dve.tensor_tensor(lexp[:, :, :], lroot[:, 1, :, :], lroot[:, 1, :, :],
                                      ALU.mult).then_inc(sm_steps, 1)
                elif k == 5:
                    dve.wait_ge(sm_steps, at)
                    dve.tensor_reduce(lmax[:, 4, :], lexp[:, :, :], AX.X, ALU.add).then_inc(sm_steps, 1)
                elif k == 6:
                    dve.wait_ge(sm_steps, at)
                    dve.reciprocal(lmax[:, 5, :], lmax[:, 4, :]).then_inc(sm_steps, 1)
                elif k == 7:
                    dve.wait_ge(top_steps, (r + 1) * TOP_STEPS)
                    dve.scalar_tensor_tensor(out=lpick[:, :, :], in0=lexp[:, :, :], scalar=1.0 / WS,
                                             in1=picks[:, :, :], op0=ALU.mult, op1=ALU.mult).then_inc(sm_steps, 1)
                elif k == 8:
                    dve.wait_ge(sm_steps, at)
                    dve.tensor_tensor(CW[:, bass.ts(r, GS * E1)].rearrange("p (s e) -> p s e", s=GS),
                                      lpick[:, :, :], over_e(lmax[:, 5, :], E1), ALU.mult).then_inc(sm_steps, 1)

            def hidden_low(m, e):
                dve.wait_ge(high_rdy, m * 4 + (e // 2 + 1))
                dve.tensor_tensor(hTl[:, e // 2 % 2, :], hT[:, e % 4, :], hTh[:, e // 2 % 2, :],
                                  ALU.subtract).then_inc(low_rdy, 1)

            def weigh(m, p):
                if p == 0:
                    hold(dve, sm_steps, (m + 1) * SM_STEPS)
                dve.wait_ge(dn_mm, m * 8 + (2 * p + 2))
                if after_first(m) or p > 1:
                    dve.wait_ge(sum_b, m * 4 + (p - 1))
                cw = CW[:, bass.ts(m, GS * E1)].rearrange("p (s e) -> p s e", s=GS)[:, :, 2 * p:2 * p + 2]
                dve.tensor_tensor(prod[:, p % 2, :, :, :],
                                  ps_dn[p % 2][:, :].rearrange("p (s k d) -> p s k d", s=GS, k=2),
                                  cw.unsqueeze(3).broadcast_to([P, GS, 2, D]), ALU.mult).then_inc(prod_rdy, 1)

            def front(i):
                step(top2, i - 5, 9)
                step(hn_low, i - 2)
                step(softmax8, i - 5, 4)
                step(top2, i - 5, 10)
                step(softmax8, i - 5, 5)
                step(top2, i - 5, 11)
                step(softmax8, i - 5, 6)
                step(top2, i - 5, 12)
                step(hidden_low, i - 5, 3)
                step(degree, i - 2)
                step(softmax8, i - 5, 7)
                step(inverse_degree, i - 2)
                step(high_half, i - 4, x2, x2_parts, x2_rdy, xsT_mm, hi2_rdy)
                step(softmax8, i - 5, 8)
                step(low_half, i - 4, x2, x2_parts, hi2_rdy, x2p_rdy)
                step(embedded, i - 2)
                step(weigh, i - 5, 0)
                step(hidden_low, i - 5, 5)
                step(stats_in, i - 2, "rnn", h1_rdy)
                step(stats_out, i - 2, "rnn")
                step(weigh, i - 5, 1)
                step(equal_tokens, i - 1, 0)
                step(top2, i - 4, 0)
                step(top2, i - 4, 1)
                step(equal_tokens, i - 1, 1)
                step(hidden_low, i - 5, 7)
                step(one_hot, i)
                step(top2, i - 4, 2)
                step(top2, i - 4, 3)
                step(equal_tokens, i - 1, 2)
                step(top2, i - 4, 4)
                step(add_states, i - 3)
                step(top2, i - 4, 5)
                step(stats_in, i - 3, "moe", h2_rdy)
                step(top2, i - 4, 6)
                step(stats_out, i - 3, "moe")
                step(equal_tokens, i - 1, 3)
                step(weigh, i - 5, 2)
                step(softmax8, i - 4, 0)
                step(top2, i - 4, 7)
                step(softmax8, i - 4, 1)
                step(hidden_low, i - 4, 1)
                step(softmax8, i - 4, 2)
                step(top2, i - 4, 8)
                step(softmax8, i - 4, 3)
                step(weigh, i - 5, 3)

            run(dve, front, 5, (prepare_up, None, prepare_down))

            def router_logits(f):
                dve.wait_ge(rlog_mm, f + 1)
                dve.scalar_tensor_tensor(out=rlog[:, :, :], in0=ps_r[:, 0:GS * E2].rearrange("p (s e) -> p s e", s=GS),
                                         scalar=1.0 / WS, in1=over_s(w("rout_b"), P, E2), op0=ALU.mult,
                                         op1=ALU.add).then_inc(rlog_rdy, 1)

            def top1(f, k):
                at = f * RT_STEPS + k
                if k == 0:
                    dve.wait_ge(rlog_rdy, f + 1)
                    dve.tensor_reduce(rmax[:, 0, :], rlog[:, :, :], AX.X, ALU.max).then_inc(rt_steps, 1)
                elif k == 1:
                    dve.wait_ge(rt_steps, at)
                    dve.tensor_tensor(req[:, :, :], rlog[:, :, :], over_e(rmax[:, 0, :], E2),
                                      ALU.is_equal).then_inc(rt_steps, 1)
                elif k == 2:
                    dve.wait_ge(rt_steps, at)
                    dve.tensor_tensor(rrank[:, :, :], req[:, :, :], rank32[:, :, :], ALU.mult).then_inc(rt_steps, 1)
                elif k == 3:
                    dve.wait_ge(rt_steps, at)
                    dve.tensor_reduce(rmax[:, 1, :], rrank[:, :, :], AX.X, ALU.max).then_inc(rt_steps, 1)
                elif k == 4:
                    dve.wait_ge(rt_steps, at)
                    wait_pos(dve, routeT_mm, f)
                    for c in range(3):
                        last = dve.tensor_tensor(route[:, :, c, :], rrank[:, :, :], over_e(rmax[:, 1, :], E2),
                                                 ALU.is_equal)
                    last.then_inc(route_rdy, 1)

            def weight_sum(a):
                dve.wait_ge(ctx_mm, a + 1)
                dve.reciprocal(rden[:, :], ps_t[:, 0:GS * (D + 1)].rearrange("p (s d) -> p s d", s=GS)[:, :, D]
                               ).then_inc(den_rdy, 1)

            def context_out(a):
                dve.wait_ge(den_rdy, a + 1)
                wait_pos(dve, h4_rdy, a)
                dve.tensor_tensor(ctxn[:, :, :], ps_t[:, 0:GS * (D + 1)].rearrange("p (s d) -> p s d", s=GS)[:, :, 0:D],
                                  over_d(rden[:, :]), ALU.mult).then_inc(ctx_rdy, 1)

            def relu_rest(f, c):
                dve.wait_ge(relu_rdy, f * 4 + (c + 1))
                dve.scalar_tensor_tensor(out=f1l[:, c, :], in0=ps_f1[c][:, :], scalar=0.0, in1=f1h[:, c, :],
                                         op0=ALU.max, op1=ALU.subtract).then_inc(rest_rdy, 1)

            def relu_y(f):
                dve.wait_ge(f2_mm, f * 4 + 4)
                wait_pos(dve, fin_rdy, f)
                dve.tensor_scalar(y[:, :], ps_x[:, 0:GD], 1.0 / (WS * WS), 0.0, ALU.mult, ALU.max).then_inc(y_rdy, 1)

            def back(i):
                step(top1, i - 4, 0)
                step(stats_in, i, "att", sum_b, 4)
                step(weight_sum, i - 2)
                step(top1, i - 4, 1)
                step(context_out, i - 2)
                step(relu_rest, i - 6, 3)
                step(stats_out, i, "att")
                step(top1, i - 4, 2)
                step(low_half, i - 3, x4, x4_parts, hi4_rdy, x4p_rdy)
                step(stats_in, i - 2, "ffn", h4_rdy)
                step(top1, i - 4, 3)
                step(stats_out, i - 2, "ffn")
                step(top1, i - 4, 4)
                step(relu_rest, i - 5, 0)
                step(relu_y, i - 6)
                step(relu_rest, i - 5, 1)
                step(router_logits, i - 3)
                step(relu_rest, i - 5, 2)

            run(dve, back, 6, (prepare_first_bias, prepare_second_bias))


def kernel(**inputs):
    import numpy as _np
    import concourse.bacc as _bacc
    from concourse import mybir as _mybir
    from concourse.bass_utils import run_bass_kernel_spmd as _run

    x = {k: _np.ascontiguousarray(v) for k, v in inputs.items()}
    P = 128
    up, down = x["L0_ffn_W1"], x["L0_ffn_W2"]
    f_up, f_down = x["L1_ffn_W1"], x["L1_ffn_W2"]

    def twice(a):
        return _np.concatenate([a, a], 0)

    def every(a):
        return _np.tile(a.reshape(1, -1), (P, 1))

    def four(a):
        return _np.tile(a, (4, 1))

    pieces = {
        "emb": x["L0_tok_emb_table"][:P],
        "w_in": twice(x["L0_tok_W_in"].T),
        "w_ih": twice(x["L0_attn_W_ih"].T),
        "w_hh": twice(x["L0_attn_W_hh"].T),
        "b_ih": twice(x["L0_attn_b_ih"].reshape(-1, 1)),
        "b_hh": twice(x["L0_attn_b_hh"].reshape(-1, 1)),
        "b_oah": every(x["L0_tok_b_oah"]),
        "w1": twice(up.transpose(1, 0, 2).reshape(64, -1)),
        "b1": x["L0_ffn_b1"].T,
        "w2": down.transpose(1, 0, 2).reshape(P, -1),
        "b2": every(x["L0_ffn_b2"]),
        "gate": twice(x["L0_ffn_gate_w"]),
        "gate_b": every(x["L0_ffn_gate_b"]),
        "rout": twice(x["L1_ffn_router_w"].T),
        "rout_b": every(x["L1_ffn_router_b"]),
        "f1": twice(f_up.transpose(1, 0, 2).reshape(64, -1)),
        "f1b": every(x["L1_ffn_b1"]),
        "f2": f_down.reshape(4, P, 64).transpose(1, 0, 2).reshape(P, -1),
        "f2b": four(x["L1_ffn_b2"]),
    }
    cols, at = {}, 0
    for name, piece in pieces.items():
        cols[name] = (at, piece.shape[1])
        at += piece.shape[1]
    cols["_total"] = at
    cols["_early"] = cols["w1"][0]
    weights = _np.ascontiguousarray(_np.concatenate(list(pieces.values()), 1))
    arrays = {
        "tok": x["x"],
        "tok_cols": _np.ascontiguousarray(x["x"].T),
        "weights": weights,
        "emb_tail": _np.tile(x["L0_tok_emb_table"][P:], (96, 1)),
    }
    nc = _bacc.Bacc("TRN2", target_bir_lowering=False, num_devices=1)
    args = [nc.dram_tensor(n, a.shape, _mybir.dt.from_np(a.dtype), kind="ExternalInput").ap() for n, a in arrays.items()]
    out = nc.dram_tensor("out", (64, 128, 64), _mybir.dt.float32, kind="ExternalOutput").ap()
    lm_tower_kernel(nc, *args, out, cols)
    r = _run(nc, [arrays], core_ids=[0])
    return r.results[0]["out"]
```
